# Optimizing a Trainium2 kernel written in Bass

```python
import numpy as np
import jax
import jax.numpy as jnp

def _softmax(x, axis=-1):
    return jax.nn.softmax(x, axis=axis)

def _gelu(x):
    return jax.nn.gelu(x, approximate=True)

def _silu(x):
    return jax.nn.silu(x)

def _sigmoid(x):
    return jax.nn.sigmoid(x)

def _layernorm(x, axis=-1, eps=1e-05):
    m = jnp.mean(x, axis=axis, keepdims=True)
    v = jnp.var(x, axis=axis, keepdims=True)
    return (x - m) / jnp.sqrt(v + eps)

def _scatter_add(tgt, idx, src, axis=0):
    return tgt.at[idx].add(src)

def _segment_sum(src, seg, n):
    return jax.ops.segment_sum(src, seg, n)
kernel_name = 'mk_xattn_ffn_d1_seqx_r8_5ab14e'

def setup_inputs(seed: int=0):
    np.random.seed(seed)
    _w = jnp.asarray

    def _rec_inputs():
        import jax
        import jax.numpy as jnp
        _rk = jax.random.key(seed)
        x = -0.000125 + 0.9999 * jax.random.normal(jax.random.fold_in(_rk, 1), (4, 256, 256), jnp.float32)
        _lenS = 256 - jax.random.randint(jax.random.fold_in(_rk, 7), (4,), 0, max(1, 256 // 4) + 1, jnp.int32)
        _lenS2 = 256 - jax.random.randint(jax.random.fold_in(_rk, 8), (4,), 0, max(1, 256 // 4) + 1, jnp.int32)
        itok_BxS_13_99985 = jax.random.randint(jax.random.fold_in(_rk, 11), (4, 256), 13, 99986, jnp.int32)
        _ctx_2048P = jax.random.normal(jax.random.fold_in(_rk, 12), (4, 16, 256), jnp.float32)
        _ctx_2048c = jax.random.dirichlet(jax.random.fold_in(_rk, 512), 0.3 * jnp.ones((16,), jnp.float32), (4, 256))
        _ctx_2048t = jnp.einsum('bsk,bkd->bsd', _ctx_2048c, _ctx_2048P)
        _ctx_2048t = _ctx_2048t * jax.lax.rsqrt(jnp.mean(jnp.square(_ctx_2048t)) + 1e-12) * 0.953939
        ctx_2048 = 6.82029e-06 + 0.0200006 * (_ctx_2048t + 0.3 * jax.random.normal(jax.random.fold_in(_rk, 612), (4, 256, 256), jnp.float32))
        return (x, itok_BxS_13_99985, ctx_2048)
    x, itok_BxS_13_99985, ctx_2048 = _rec_inputs()

    def _L0_xattn_setup():
        import jax, jax.numpy as jnp
        import numpy as np
        B, S, D = (4, 512, 256)
        E = 4
        F = 1024 // E
        VOCAB = 12500
        key = jax.random.key(seed)
        k1, k2, k3, k4, k5 = jax.random.split(key, 5)
        hidden_states = jax.random.normal(k1, (B, S, D), dtype=jnp.float32)
        token_ids = jax.random.randint(k2, (B, S), 0, VOCAB, dtype=jnp.int64)
        Wg = jax.random.normal(k3, (E, F, D), dtype=jnp.float32) * 0.02
        Wu = jax.random.normal(k4, (E, F, D), dtype=jnp.float32) * 0.02
        Wd = jax.random.normal(k5, (E, D, F), dtype=jnp.float32) * 0.02
        return {'hidden_states': hidden_states, 'token_ids': token_ids, 'Wg': Wg, 'Wu': Wu, 'Wd': Wd}
    _L0_xattn_all = _L0_xattn_setup()
    _L0_xattn_in = {k: v for k, v in _L0_xattn_all.items() if k in ()}
    del _L0_xattn_all

    def _L0_ffn_setup():
        import jax, jax.numpy as jnp
        import numpy as np
        BLOCK_SIZE = 32
        HIDDEN_SIZE = 256
        MLP_DIM = 2048
        NVFP4_LUT = jnp.array([0.0, 0.5, 1.0, 1.5, 2.0, 3.0, 4.0, 6.0, 0.0, -0.5, -1.0, -1.5, -2.0, -3.0, -4.0, -6.0], dtype=jnp.float32)

        def dequant_nvfp4(W_packed, scales, block=BLOCK_SIZE):
            N = W_packed.shape[0]
            low = W_packed & 15
            high = W_packed >> 4 & 15
            idx = jnp.stack([low, high], axis=-1).reshape(N, -1)
            vals = NVFP4_LUT[idx]
            K = vals.shape[1]
            vals = vals.reshape(N, K // block, block) * scales[:, :, None]
            return vals.reshape(N, K)
        key = jax.random.key(seed)
        ks = jax.random.split(key, 7)
        x = jax.random.normal(ks[0], (4, 32, HIDDEN_SIZE), dtype=jnp.float32)
        gate_W_packed = jax.random.randint(ks[1], (MLP_DIM, HIDDEN_SIZE // 2), 0, 32, dtype=jnp.int32)
        gate_scales = jax.random.uniform(ks[2], (MLP_DIM, HIDDEN_SIZE // BLOCK_SIZE), dtype=jnp.float32) * 0.1 + 0.001
        up_W_packed = jax.random.randint(ks[3], (MLP_DIM, HIDDEN_SIZE // 2), 0, 32, dtype=jnp.int32)
        up_scales = jax.random.uniform(ks[4], (MLP_DIM, HIDDEN_SIZE // BLOCK_SIZE), dtype=jnp.float32) * 0.1 + 0.001
        down_W_packed = jax.random.randint(ks[5], (HIDDEN_SIZE, MLP_DIM // 2), 0, 32, dtype=jnp.int32)
        down_scales = jax.random.uniform(ks[6], (HIDDEN_SIZE, MLP_DIM // BLOCK_SIZE), dtype=jnp.float32) * 0.1 + 0.001
        return {'x': x, 'gate_W_packed': gate_W_packed, 'gate_scales': gate_scales, 'up_W_packed': up_W_packed, 'up_scales': up_scales, 'down_W_packed': down_W_packed, 'down_scales': down_scales}
    _L0_ffn_all = _L0_ffn_setup()
    _L0_ffn_in = {k: v for k, v in _L0_ffn_all.items() if k in ('gate_W_packed', 'gate_scales', 'up_W_packed', 'up_scales', 'down_W_packed', 'down_scales')}
    del _L0_ffn_all
    return {'x': x, 'itok_BxS_13_99985': itok_BxS_13_99985, 'ctx_2048': ctx_2048, 'L0_ffn_gate_W_packed': _L0_ffn_in['gate_W_packed'], 'L0_ffn_gate_scales': _L0_ffn_in['gate_scales'], 'L0_ffn_up_W_packed': _L0_ffn_in['up_W_packed'], 'L0_ffn_up_scales': _L0_ffn_in['up_scales'], 'L0_ffn_down_W_packed': _L0_ffn_in['down_W_packed'], 'L0_ffn_down_scales': _L0_ffn_in['down_scales']}

def reference(x, itok_BxS_13_99985, ctx_2048, L0_ffn_gate_W_packed, L0_ffn_gate_scales, L0_ffn_up_W_packed, L0_ffn_up_scales, L0_ffn_down_W_packed, L0_ffn_down_scales):
    import jax
    import jax.numpy as jnp

    def _L0_xattn_ref(hidden_states, token_ids, Wg, Wu, Wd):
        import jax, jax.numpy as jnp
        import numpy as np
        B, S, D = (4, 512, 256)
        E = 4
        F = 1024 // E
        VOCAB = 12500
        tokens_per_expert = VOCAB // E
        tid = jnp.clip(token_ids, 0, VOCAB - 1)
        expert_ids = jnp.minimum(tid // tokens_per_expert, E - 1)
        out = jnp.zeros_like(hidden_states)
        for e in range(E):
            g = jax.nn.silu(jnp.einsum('bsd,fd->bsf', hidden_states, Wg[e]))
            u = jnp.einsum('bsd,fd->bsf', hidden_states, Wu[e])
            y = jnp.einsum('bsf,df->bsd', g * u, Wd[e])
            out = jnp.where((expert_ids == e)[..., None], y, out)
        return out

    def _L0_ffn_ref(x, gate_W_packed, gate_scales, up_W_packed, up_scales, down_W_packed, down_scales):
        import jax, jax.numpy as jnp
        import numpy as np
        BLOCK_SIZE = 32
        HIDDEN_SIZE = 256
        MLP_DIM = 2048
        NVFP4_LUT = jnp.array([0.0, 0.5, 1.0, 1.5, 2.0, 3.0, 4.0, 6.0, 0.0, -0.5, -1.0, -1.5, -2.0, -3.0, -4.0, -6.0], dtype=jnp.float32)

        def dequant_nvfp4(W_packed, scales, block=BLOCK_SIZE):
            N = W_packed.shape[0]
            low = W_packed & 15
            high = W_packed >> 4 & 15
            idx = jnp.stack([low, high], axis=-1).reshape(N, -1)
            vals = NVFP4_LUT[idx]
            K = vals.shape[1]
            vals = vals.reshape(N, K // block, block) * scales[:, :, None]
            return vals.reshape(N, K)
        B, S, H = x.shape
        xt = x.reshape(B * S, H)
        Wg = dequant_nvfp4(gate_W_packed, gate_scales)
        Wu = dequant_nvfp4(up_W_packed, up_scales)
        Wd = dequant_nvfp4(down_W_packed, down_scales)
        gate = jnp.einsum('th,nh->tn', xt, Wg)
        up = jnp.einsum('th,nh->tn', xt, Wu)
        gelu = jnp.tanh(0.7978845608028654 * (gate + 0.044715 * gate ** 3)) * gate * 0.5 + gate * 0.5
        inter = gelu * up
        out = jnp.einsum('tn,hn->th', inter, Wd)
        return out.reshape(B, S, H)
    x = x + _L0_xattn_ref(_layernorm(x, axis=-1), itok_BxS_13_99985, ctx_2048, ctx_2048, ctx_2048)
    x = x + _L0_ffn_ref(_layernorm(x, axis=-1), L0_ffn_gate_W_packed, L0_ffn_gate_scales, L0_ffn_up_W_packed, L0_ffn_up_scales, L0_ffn_down_W_packed, L0_ffn_down_scales)
    return x

_drawn_inputs = setup_inputs


def setup_inputs(seed=0):
    import zlib

    import numpy as np

    out = dict(_drawn_inputs(seed))
    spreads = {}
    factors = {}
    for name, (base, spread) in spreads.items():
        noise = np.random.default_rng([zlib.crc32(name.encode()), seed]).standard_normal(out[name].shape)
        drawn = base * np.exp(spread * noise) if base else spread * noise
        out[name] = jnp.asarray(drawn.astype(out[name].dtype))
    for name, factor in factors.items():
        out[name] = (out[name] * factor).astype(out[name].dtype)
    return out
```

```python
import concourse.bass as bass
from concourse import mybir
from contextlib import ExitStack

P = 128
TOKENS, D = 1024, 256
TT = TOKENS // P
KT = D // P
E = 4
EF = E * 256
VOCAB = 12500
PER_EXPERT = VOCAB // E
EPS = 1e-5
N = 2048
NT = N // P
BLOCK = 32
NPAIR = NT // 2
CHUNK = 512
CT = CHUNK // P
FP4_SHIFT = 64.0


def xattn_ffn(nc, x, tok, ctx_w, gate_w, gate_s, up_w, up_s, down_w, down_s, out):
    fp32, f32r = mybir.dt.float32, mybir.dt.float32r
    i32, u16, fp8 = mybir.dt.int32, mybir.dt.uint16, mybir.dt.float8e4
    ALU, ACT = mybir.AluOpType, mybir.ActivationFunctionType
    ds = bass.ds

    stack = ExitStack()
    with stack:
        def sb(name, shape, dt):
            return stack.enter_context(nc.sbuf_tensor(name, shape, dt))

        def sem(name):
            return stack.enter_context(nc.semaphore(name))

        x_sb = sb("x_sb", [P, TT, D], fp32)
        tok_sb = sb("tok_sb", [P, TT], i32)
        below = sb("below", [P, 2, TT], fp32)
        mask = sb("mask", [P, E, TT], fp32)
        ident = sb("ident", [P, P], fp32)
        neg_half = sb("neg_half", [P, TT], fp32)
        stats = sb("stats", [P, TT, 6], fp32)
        ln_tmp = sb("ln_tmp", [P, 5, TT], fp32)
        mean = sb("mean", [P, TT], fp32)
        var = sb("var", [P, TT], fp32)
        rstd = sb("rstd", [P, TT], fp32)
        ctx_sb = sb("ctx_sb", [P, TT, D], fp32)
        h2_sb = ctx_sb[:, 0:CT, :]
        outT_sb = ctx_sb[:, CT:TT, :].rearrange("p a b -> p (a b)").rearrange("p (h t) -> p h t", h=KT)
        cT_hi = sb("cT_hi", [P, KT, EF], f32r)
        cT_lo = sb("cT_lo", [P, KT, EF], f32r)
        h_sb = sb("h_sb", [P, 2, D], fp32)
        hT_hi = sb("hT_hi", [P, 2, D], f32r)
        hT_lo = sb("hT_lo", [P, 2, D], f32r)
        act_sb = sb("act_sb", [P, 2, CHUNK], fp32)
        prod_sb = sb("prod_sb", [P, 2, CHUNK], fp32)
        prodT_hi = sb("prodT_hi", [P, 2, CHUNK], f32r)
        prodT_lo = sb("prodT_lo", [P, 2, CHUNK], f32r)
        gu_pk = sb("gu_pk", [P, 2, NT * 128], i32)
        d_pk = sb("d_pk", [P, KT, N // 2], i32)
        gu_sc = sb("gu_sc", [P, 2, NPAIR, 16], fp32)
        d_sc = sb("d_sc", [P, KT * N // BLOCK], fp32)
        d_scx = sb("d_scx", [P, KT, 128], fp32)
        code_hi = sb("code_hi", [P, 512], u16)
        code_lh = sb("code_lh", [P, 512], u16)
        code_mag = sb("code_mag", [P, 512], u16)
        code_sgn = sb("code_sgn", [P, 512], u16)
        gu_code = sb("gu_code", [P, 512], u16)
        d_code = sb("d_code", [P, 256], u16)
        gu_nat = sb("gu_nat", [P, 2, 2, D], fp32)
        d_nat = sb("d_nat", [P, KT, 2, P], fp32)
        wgu_hi = sb("wgu_hi", [P, 2, KT, N], f32r)
        wgu_lo = sb("wgu_lo", [P, 2, KT, N], f32r)
        wd_hi = sb("wd_hi", [P, NT * D], f32r)
        wd_lo = sb("wd_lo", [P, NT * D], f32r)
        h2T_hi = sb("h2T_hi", [P, KT, TOKENS], f32r)
        h2T_lo = sb("h2T_lo", [P, KT, TOKENS], f32r)

        bank = [stack.enter_context(nc.psum_tensor(f"bank{b}", [P, 512], fp32)) for b in range(8)]
        ps_z, ps_aT, ps_y = bank[0:2], bank[2:4], bank[4:6]
        ps_gate, ps_up, ps_o = (bank[0], bank[2]), (bank[1], bank[3]), bank[4:6]
        ps_h, ps_w = bank[6], bank[7]
        ps_out = (bank[6], bank[7])

        s_tok, s_x01, s_x27 = sem("s_tok"), sem("s_x01"), sem("s_x27")
        s_ctx = [sem("s_ctx0"), sem("s_ctx1")]
        s_gusc, s_dsc = sem("s_gusc"), sem("s_dsc")
        s_gupk = [sem("s_gupk0"), sem("s_gupk1")]
        s_dpk = sem("s_dpk")
        s_out = [sem(f"s_out{n}") for n in range(4)]
        pool_const = sem("pool_const")
        dsc_ready = sem("dsc_ready")
        mask_ready = sem("mask_ready")
        ln_step = sem("ln_step")
        var_ready = sem("var_ready")
        rstd_ready = sem("rstd_ready")
        cT_ps, cT_hi_ok, cT_lo_ok = sem("cT_ps"), sem("cT_hi_ok"), sem("cT_lo_ok")
        h_ready = sem("h_ready")
        hT_ps, hT_hi_ok, hT_lo_ok = sem("hT_ps"), sem("hT_hi_ok"), sem("hT_lo_ok")
        z_ready = sem("z_ready")
        silu_ready = sem("silu_ready")
        a_ready = sem("a_ready")
        aT_ps, aT_hi_ok, aT_lo_ok = sem("aT_ps"), sem("aT_hi_ok"), sem("aT_lo_ok")
        y_ready = sem("y_ready")
        x1_ready = sem("x1_ready")
        gu_step, d_step = sem("gu_step"), sem("d_step")
        gu_codes, d_codes = sem("gu_codes"), sem("d_codes")
        gu_nat_ok, d_nat_ok = sem("gu_nat_ok"), sem("d_nat_ok")
        w_ps, w_hi_ok, w_lo_ok = sem("w_ps"), sem("w_hi_ok"), sem("w_lo_ok")
        h2_ready = sem("h2_ready")
        h2_ps, h2_hi_ok, h2_lo_ok = sem("h2_ps"), sem("h2_hi_ok"), sem("h2_lo_ok")
        gate_ready, up_ready = sem("gate_ready"), sem("up_ready")
        gelu_ready = sem("gelu_ready")
        inter_ready = sem("inter_ready")
        i_hi_ok, i_lo_ok = sem("i_hi_ok"), sem("i_lo_ok")
        o_ready = sem("o_ready")
        outT_ok = sem("outT_ok")
        out_ps = sem("out_ps")
        res_ready = sem("res_ready")

        HALF = NPAIR // 2

        def piece_gu(t, m):
            return 2 * t + m

        def piece_gu_late(t, m):
            return 2 * HALF + 3 * t + 1 + m

        def piece_d_early(t):
            return 2 * HALF + 3 * t

        def piece_d_late(t):
            return 2 * HALF + 3 * HALF + (t - HALF)

        def piece_d(t):
            return piece_d_early(t) if t < HALF else piece_d_late(t)

        x_v = x.rearrange("(p j) d -> p j d", j=TT)
        out_v = out.rearrange("(p j) d -> p j d", j=TT)
        block = stack.enter_context(nc.Block())

        @block.sync
        def _(sp):
            sp.dma_start(x_sb[:, 0:2, :], x_v[:, 0:2, :]).then_inc(s_x01, 16)
            sp.dma_start(tok_sb[:, :], tok.rearrange("(p j) -> p j", j=TT)).then_inc(s_tok, 16)
            for half in range(2):
                sp.dma_start(ctx_sb[:, 4 * half:4 * half + 4, :],
                             ctx_w.rearrange("(b p) c -> p b c", p=P)[:, 4 * half:4 * half + 4, :]
                             ).then_inc(s_ctx[half], 16)
            sp.dma_start(x_sb[:, 2:TT, :], x_v[:, 2:TT, :]).then_inc(s_x27, 16)
            for m, s in enumerate((gate_s, up_s)):
                sp.dma_start(gu_sc[:, m, :, :],
                             s.rearrange("(p g i) b -> p g (i b)", g=NPAIR, i=2)).then_inc(s_gusc, 16)
            for part in range(2):
                cols = slice(part * N // 2, (part + 1) * N // 2)
                for m, w in enumerate((gate_w, up_w)):
                    sp.dma_start(gu_pk[:, m, cols],
                                 w.rearrange("(p i) c -> p (i c)", i=NT)[:, cols]).then_inc(s_gupk[part], 16)
            sp.dma_start(d_sc[:, :].rearrange("p (h b) -> p h b", h=KT),
                         down_s.rearrange("(h p) b -> p h b", p=P)).then_inc(s_dsc, 16)
            sp.dma_start(d_pk[:, :, :], down_w.rearrange("(h p) c -> p h c", p=P)).then_inc(s_dpk, 16)
            for n in range(4):
                sp.wait_ge(res_ready, n + 1)
                sp.dma_start(out_v[:, 2 * n:2 * n + 2, :], x_sb[:, 2 * n:2 * n + 2, :]).then_inc(s_out[n], 16)
            for n in range(4):
                sp.wait_ge(s_out[n], 16)

        @block.gpsimd
        def _(pool):
            nc.gpsimd.memset(ident[:, :], 0.0).then_inc(pool_const, 1)
            nc.gpsimd.memset(neg_half[:, :], -0.5).then_inc(pool_const, 1)
            pool.wait_ge(pool_const, 2)
            nc.gpsimd.affine_select(out=ident[:, :], in_=ident[:, :], compare_op=ALU.not_equal, fill=1.0,
                                    base=0, pattern=[[-1, P]], channel_multiplier=1).then_inc(pool_const, 1)

            def inv_std(batch, t0, n):
                pool.wait_ge(var_ready, batch + 1)
                nc.gpsimd.tensor_tensor(rstd[:, t0:t0 + n], var[:, t0:t0 + n], neg_half[:, t0:t0 + n],
                                        ALU.pow).then_inc(rstd_ready, 1)

            def dequant_gu(g):
                pool.wait_ge(gu_codes, g + 1)
                for m in range(2):
                    nc.gpsimd.tensor_tensor(
                        gu_nat[:, m, :, :].rearrange("p i (b c) -> p (i b) c", c=BLOCK),
                        gu_code[:, 256 * m:256 * (m + 1)].bitcast(fp8).rearrange("p (b c) -> p b c", c=BLOCK),
                        gu_sc[:, m, g, :].unsqueeze(2).to_broadcast([P, 16, BLOCK]),
                        ALU.mult).then_inc(gu_nat_ok, 1)

            def dequant_d(g):
                pool.wait_ge(d_codes, g + 1)
                nc.gpsimd.tensor_tensor(
                    d_nat[:, :, :, :].rearrange("p h i q -> p h q i"),
                    d_code[:, :].bitcast(fp8).rearrange("p (h q i) -> p h q i", h=KT, i=2),
                    d_scx[:, :, :].unsqueeze(3).to_broadcast([P, KT, P, 2]),
                    ALU.mult).then_inc(d_nat_ok, 1)

            inv_std(0, 0, 2)
            inv_std(1, 2, TT - 2)
            pool.wait_ge(s_gusc, 32)
            nc.gpsimd.tensor_scalar(gu_sc[:, :, :, :].rearrange("p m g b -> p (m g b)"),
                                    gu_sc[:, :, :, :].rearrange("p m g b -> p (m g b)"),
                                    FP4_SHIFT, 1.0, ALU.mult, ALU.mult).then_inc(dsc_ready, 1)
            pool.wait_ge(s_dsc, 16)
            nc.gpsimd.tensor_scalar(d_scx[:, :, :].rearrange("p h (b s) -> p (h b) s", s=2),
                                    d_sc[:, :].unsqueeze(2).to_broadcast([P, KT * N // BLOCK, 2]),
                                    FP4_SHIFT, 1.0, ALU.mult, ALU.mult).then_inc(dsc_ready, 1)
            pool.wait_ge(dsc_ready, 2)
            for g in range(HALF):
                dequant_gu(g)
            inv_std(2, 0, CT)
            dequant_gu(HALF)
            dequant_d(0)
            for t in range(HALF - 1):
                dequant_gu(t + HALF + 1)
                dequant_d(t + 1)
            dequant_d(HALF)
            inv_std(3, CT, CT)
            for t in range(HALF + 1, NPAIR):
                dequant_d(t)

        def products(psum, terms, first=True, last=True):
            n = 0
            for w_hi, w_lo, m_hi, m_lo in terms:
                for w, m in ((w_hi, m_hi), (w_hi, m_lo), (w_lo, m_hi)):
                    mm = nc.tensor.matmul(psum, w, m, start=first and n == 0,
                                          stop=last and n == 3 * len(terms) - 1)
                    n += 1
            return mm

        @block.tensor
        def _(pe):
            def transpose_h(j, u):
                pe.wait_ge(h_ready, j + 1)
                for kt in range(KT):
                    mm = nc.tensor.transpose(ps_h[:, kt * P:(kt + 1) * P],
                                             h_sb[:, u, kt * P:(kt + 1) * P], ident[:, :])
                mm.then_inc(hT_ps, 1)

            def expert_in(j, u):
                pe.wait_ge(hT_lo_ok, j + 1)
                for half in range(2):
                    cols = slice(half * 512, half * 512 + 512)
                    products(ps_z[half][:, :],
                             [(hT_hi[:, u, kt * P:(kt + 1) * P], hT_lo[:, u, kt * P:(kt + 1) * P],
                               cT_hi[:, kt, cols], cT_lo[:, kt, cols]) for kt in range(KT)]
                             ).then_inc(z_ready, 1)

            def transpose_a(j):
                for half in range(2):
                    pe.wait_ge(a_ready, 2 * j + half + 1)
                    for b in range(4):
                        mm = nc.tensor.transpose(ps_aT[half][:, b * P:(b + 1) * P],
                                                 prod_sb[:, half, b * P:(b + 1) * P], ident[:, :])
                    mm.then_inc(aT_ps, 1)

            def expert_out(j, u):
                for half in range(2):
                    pe.wait_ge(aT_lo_ok, 2 * j + half + 1)
                    terms = []
                    for b in range(4):
                        e, kt = 2 * half + b // KT, b % KT
                        cols = slice(b * P, (b + 1) * P)
                        terms.append((prodT_hi[:, half, cols], prodT_lo[:, half, cols],
                                      cT_hi[:, kt, e * D:(e + 1) * D], cT_lo[:, kt, e * D:(e + 1) * D]))
                    mm = products(ps_y[u][:, 0:D], terms, first=half == 0, last=half == 1)
                mm.then_inc(y_ready, 1)

            def transpose_gu(g, m, piece=None):
                if piece is not None:
                    pe.wait_ge(w_lo_ok, piece)
                pe.wait_ge(gu_nat_ok, 2 * g + m + 1)
                for kt in range(KT):
                    for i in range(2):
                        c = (2 * kt + i) * P
                        mm = nc.tensor.transpose(ps_w[:, c:c + P], gu_nat[:, m, i, kt * P:(kt + 1) * P],
                                                 ident[:, :])
                mm.then_inc(w_ps, 1)

            def transpose_d(g, piece):
                pe.wait_ge(w_lo_ok, piece)
                pe.wait_ge(d_nat_ok, g + 1)
                for i in range(2):
                    for hb in range(KT):
                        c = (2 * i + hb) * P
                        mm = nc.tensor.transpose(ps_w[:, c:c + P], d_nat[:, hb, i, :], ident[:, :])
                mm.then_inc(w_ps, 1)

            def transpose_h2(c, kt, psum, lo_taken=0):
                pe.wait_ge(h2_ready, c + 1)
                if lo_taken:
                    pe.wait_ge(h2_lo_ok, lo_taken)
                for j in range(CT):
                    mm = nc.tensor.transpose(psum[:, j * P:(j + 1) * P],
                                             h2_sb[:, j, kt * P:(kt + 1) * P], ident[:, :])
                mm.then_inc(h2_ps, 1)

            pe.wait_ge(pool_const, 3)
            transpose_h(0, 0)
            for half in range(2):
                pe.wait_ge(s_ctx[half], 16)
                for kt in range(KT):
                    for b in range(4):
                        mm = nc.tensor.transpose(bank[2 * half + kt][:, b * P:(b + 1) * P],
                                                 ctx_sb[:, 4 * half + b, kt * P:(kt + 1) * P], ident[:, :])
                    mm.then_inc(cT_ps, 1)
            pe.wait_ge(cT_lo_ok, 4)
            expert_in(0, 0)
            transpose_h(1, 1)

            def layer1_step(p, u, w_piece_wait):
                j = 2 * p + u
                transpose_a(j)
                expert_in(j + 1, 1 - u)
                transpose_h(j + 2, u)
                expert_out(j, u)
                transpose_gu(p, u, 2 * p + 1 if w_piece_wait else None)

            with pe.Fori(0, TT // 2 - 1) as p:
                layer1_step(p, 0, False)
                layer1_step(p, 1, True)

            transpose_a(TT - 2)
            expert_in(TT - 1, 1)
            expert_out(TT - 2, 0)
            transpose_gu(HALF - 1, 0, piece_gu(HALF - 1, 0))
            transpose_a(TT - 1)
            transpose_h2(0, 0, ps_h)
            expert_out(TT - 1, 1)
            transpose_gu(HALF - 1, 1, piece_gu(HALF - 1, 1))
            transpose_h2(0, 1, ps_h, lo_taken=1)

            def gate_up(n):
                c, i = n // NT, n % NT
                toks = slice(c * CHUNK, (c + 1) * CHUNK)
                for m, (psum, ready) in enumerate(((ps_gate, gate_ready), (ps_up, up_ready))):
                    products(psum[n % 2][:, :],
                             [(wgu_hi[:, m, kt, i * P:(i + 1) * P], wgu_lo[:, m, kt, i * P:(i + 1) * P],
                               h2T_hi[:, kt, toks], h2T_lo[:, kt, toks]) for kt in range(KT)]
                             ).then_inc(ready, 1)

            def down(n):
                i = n % NT
                pe.wait_ge(i_lo_ok, n + 1)
                for hb in range(KT):
                    c = i * D + hb * P
                    mm = products(ps_o[hb][:, :], [(wd_hi[:, c:c + P], wd_lo[:, c:c + P],
                                                    prodT_hi[:, n % 2, :], prodT_lo[:, n % 2, :])],
                                  first=i == 0, last=i == NT - 1)
                    if i == NT - 1:
                        mm.then_inc(o_ready, 1)

            def transpose_out(c):
                pe.wait_ge(outT_ok, KT * (c + 1))
                for pair in range(2):
                    for j in range(2):
                        for hb in range(KT):
                            t = (2 * pair + j) * P
                            mm = nc.tensor.transpose(ps_out[pair][:, (2 * j + hb) * P:(2 * j + hb + 1) * P],
                                                     outT_sb[:, hb, t:t + P], ident[:, :])
                    mm.then_inc(out_ps, 1)

            pe.wait_ge(h2_lo_ok, 2)
            pe.wait_ge(w_lo_ok, 2 * HALF)
            for t in range(NPAIR):
                if t >= HALF:
                    pe.wait_ge(w_lo_ok, piece_gu_late(t - HALF, 1) + 1)
                gate_up(2 * t)
                transpose_d(t, piece_d(t))
                if t > 0:
                    down(2 * t - 1)
                if t < HALF:
                    transpose_gu(t + HALF, 0, piece_gu_late(t, 0))
                if t == NPAIR - 1:
                    pe.wait_ge(w_lo_ok, piece_d(t) + 1)
                    transpose_h2(1, 0, ps_h)
                    transpose_h2(1, 1, ps_w)
                gate_up(2 * t + 1)
                if t < HALF:
                    transpose_gu(t + HALF, 1, piece_gu_late(t, 1))
                pe.wait_ge(w_lo_ok, piece_d(t) + 1)
                down(2 * t)
            pe.wait_ge(h2_lo_ok, 4)
            for n in range(NT, 2 * NT):
                gate_up(n)
                if n == NT + 1:
                    transpose_out(0)
                down(n - 1)
            down(2 * NT - 1)
            transpose_out(1)

        @block.scalar
        def _(act):
            def hi_part(dst, src):
                return nc.scalar.activation(dst, src, ACT.Copy)

            def hi_h(j, u):
                act.wait_ge(hT_ps, j + 1)
                hi_part(hT_hi[:, u, :], ps_h[:, 0:D]).then_inc(hT_hi_ok, 1)

            def silu(j):
                for half in range(2):
                    act.wait_ge(z_ready, 2 * j + half + 1)
                    for k in range(2):
                        e = 2 * half + k
                        op = nc.scalar.activation(act_sb[:, half, k * D:(k + 1) * D],
                                                  ps_z[half][:, k * D:(k + 1) * D], ACT.Silu,
                                                  scale=mask[:, e, ds(j, 1)])
                    op.then_inc(silu_ready, 1)

            def hi_a(j):
                for half in range(2):
                    act.wait_ge(aT_ps, 2 * j + half + 1)
                    hi_part(prodT_hi[:, half, :], ps_aT[half][:, :]).then_inc(aT_hi_ok, 1)

            def hi_gu(g, m, piece):
                act.wait_ge(w_ps, piece + 1)
                hi_part(wgu_hi[:, m, :, ds(g * D, D)],
                        ps_w[:, :].rearrange("p (k n) -> p k n", k=KT)).then_inc(w_hi_ok, 1)

            def hi_d(g, piece):
                act.wait_ge(w_ps, piece + 1)
                hi_part(wd_hi[:, ds(g * 2 * D, 2 * D)], ps_w[:, :]).then_inc(w_hi_ok, 1)

            def hi_h2(c, kt, psum):
                act.wait_ge(h2_ps, 2 * c + kt + 1)
                hi_part(h2T_hi[:, kt, c * CHUNK:(c + 1) * CHUNK], psum[:, :]).then_inc(h2_hi_ok, 1)

            def gelu(n, u):
                act.wait_ge(gate_ready, n + 1)
                nc.scalar.activation(act_sb[:, u, :], ps_gate[u][:, :],
                                     ACT.Gelu_apprx_tanh).then_inc(gelu_ready, 1)

            def hi_inter(n, u):
                act.wait_ge(inter_ready, n + 1)
                hi_part(prodT_hi[:, u, :], prod_sb[:, u, :]).then_inc(i_hi_ok, 1)

            def take_out(c):
                for hb in range(KT):
                    act.wait_ge(o_ready, KT * c + hb + 1)
                    nc.scalar.copy(outT_sb[:, hb, :], ps_o[hb][:, :]).then_inc(outT_ok, 1)

            hi_h(0, 0)
            for half in range(2):
                for kt in range(KT):
                    act.wait_ge(cT_ps, 2 * half + kt + 1)
                    hi_part(cT_hi[:, kt, half * 512:half * 512 + 512],
                            bank[2 * half + kt][:, :]).then_inc(cT_hi_ok, 1)
            act.wait_ge(mask_ready, 1)
            silu(0)
            hi_h(1, 1)
            with act.Fori(0, TT // 2 - 1) as p:
                for u in range(2):
                    hi_a(2 * p + u)
                    silu(2 * p + u + 1)
                    hi_h(2 * p + u + 2, u)
                    hi_gu(p, u, 2 * p + u)
            hi_a(TT - 2)
            silu(TT - 1)
            hi_gu(HALF - 1, 0, piece_gu(HALF - 1, 0))
            hi_a(TT - 1)
            hi_h2(0, 0, ps_h)
            hi_gu(HALF - 1, 1, piece_gu(HALF - 1, 1))
            hi_h2(0, 1, ps_h)

            def chunk0_pair(t, early, c1=False):
                gelu(2 * t, 0)
                hi_d(t, piece_d_early(t) if early else piece_d_late(t))
                hi_inter(2 * t, 0)
                if early:
                    hi_gu(t + HALF, 0, piece_gu_late(t, 0))
                if c1:
                    hi_h2(1, 0, ps_h)
                    hi_h2(1, 1, ps_w)
                gelu(2 * t + 1, 1)
                if early:
                    hi_gu(t + HALF, 1, piece_gu_late(t, 1))
                hi_inter(2 * t + 1, 1)

            with act.Fori(0, HALF) as t:
                chunk0_pair(t, True)
            with act.Fori(HALF, NPAIR - 1) as t:
                chunk0_pair(t, False)
            chunk0_pair(NPAIR - 1, False, c1=True)

            gelu(NT, 0)
            hi_inter(NT, 0)
            take_out(0)
            gelu(NT + 1, 1)
            hi_inter(NT + 1, 1)
            with act.Fori(NPAIR + 1, 2 * NPAIR) as t:
                for u in range(2):
                    gelu(2 * t + u, u)
                    hi_inter(2 * t + u, u)
            take_out(1)

        @block.vector
        def _(dve):
            tt, ts, stt = nc.vector.tensor_tensor, nc.vector.tensor_scalar, nc.vector.scalar_tensor_tensor
            steps = [0]

            def lo_part(dst, src, hi):
                return tt(dst, src, hi.bitcast(fp32), ALU.subtract)

            def ln_stats(t0, n):
                if n > 2:
                    with dve.Fori(t0, t0 + n) as j:
                        nc.vector.bn_stats(stats[:, ds(j, 1), :], x_sb[:, ds(j, 1), :]).then_inc(ln_step, 1)
                else:
                    for j in range(t0, t0 + n):
                        nc.vector.bn_stats(stats[:, j, :], x_sb[:, j, :]).then_inc(ln_step, 1)
                steps[0] += n
                r = slice(t0, t0 + n)
                mean_e, m2_e, mean_o, m2_o = (stats[:, r, k] for k in (1, 2, 4, 5))
                both, diff, m2, m2_both, between = (ln_tmp[:, k, r] for k in range(5))
                dve.wait_ge(ln_step, steps[0])
                tt(both, mean_e, mean_o, ALU.add).then_inc(ln_step, 1)
                tt(diff, mean_e, mean_o, ALU.subtract).then_inc(ln_step, 1)
                ts(m2, m2_e, 1.0 / D, EPS, ALU.mult, ALU.add).then_inc(ln_step, 1)
                dve.wait_ge(ln_step, steps[0] + 3)
                ts(mean[:, r], both, 0.5, None, ALU.mult).then_inc(ln_step, 1)
                stt(between, diff, 0.25, diff, ALU.mult, ALU.mult).then_inc(ln_step, 1)
                stt(m2_both, m2_o, 1.0 / D, m2, ALU.mult, ALU.add).then_inc(ln_step, 1)
                dve.wait_ge(ln_step, steps[0] + 6)
                tt(var[:, r], m2_both, between, ALU.add).then_inc(var_ready, 1)
                steps[0] += 6

            def normalise(dst, j):
                return ts(dst, x_sb[:, ds(j, 1), :], mean[:, ds(j, 1)], rstd[:, ds(j, 1)],
                          ALU.subtract, ALU.mult)

            def lo_h(j, u):
                dve.wait_ge(hT_hi_ok, j + 1)
                lo_part(hT_lo[:, u, :], ps_h[:, 0:D], hT_hi[:, u, :]).then_inc(hT_lo_ok, 1)

            def gated(j):
                for half in range(2):
                    dve.wait_ge(silu_ready, 2 * j + half + 1)
                    tt(prod_sb[:, half, :], act_sb[:, half, :], ps_z[half][:, :],
                       ALU.mult).then_inc(a_ready, 1)

            def lo_a(j):
                for half in range(2):
                    dve.wait_ge(aT_hi_ok, 2 * j + half + 1)
                    lo_part(prodT_lo[:, half, :], ps_aT[half][:, :], prodT_hi[:, half, :]).then_inc(aT_lo_ok, 1)

            def residual1(j, u):
                dve.wait_ge(y_ready, j + 1)
                tt(x_sb[:, ds(j, 1), :], x_sb[:, ds(j, 1), :], ps_y[u][:, 0:D], ALU.add).then_inc(x1_ready, 1)

            def decode(pk, n, shape, out_code, step, done, g):
                def v(tensor):
                    return tensor[:, 0:n].rearrange(shape[0], **shape[1])
                nib_hi, nib, mag, sgn = (v(t) for t in (code_hi, code_lh, code_mag, code_sgn))
                shl, land, lor = ALU.logical_shift_left, ALU.bitwise_and, ALU.bitwise_or
                ts(nib_hi, pk, 4, 0x0f00, shl, land).then_inc(step, 1)
                dve.wait_ge(step, 4 * g + 1)
                stt(nib, pk, 0x000f, nib_hi, land, lor).then_inc(step, 1)
                dve.wait_ge(step, 4 * g + 2)
                ts(code_mag[:, 0:n], code_lh[:, 0:n], 2, 0x1c1c, shl, land).then_inc(step, 1)
                ts(code_sgn[:, 0:n], code_lh[:, 0:n], 4, 0x8080, shl, land).then_inc(step, 1)
                dve.wait_ge(step, 4 * g + 4)
                tt(out_code, code_mag[:, 0:n], code_sgn[:, 0:n], lor).then_inc(done, 1)

            gu_half = gu_pk[:, :, :].bitcast(u16).rearrange("p m (g c two) -> p m g c two", g=NPAIR, two=2)
            d_half = d_pk[:, :, :].bitcast(u16).rearrange("p h (q g two) -> p h g q two", g=NPAIR, two=2)

            def decode_gu(g):
                decode(gu_half[:, :, ds(g, 1), :, 0], 512, ("p (m o c) -> p m o c", dict(m=2, o=1)),
                       gu_code[:, :], gu_step, gu_codes, g)

            def decode_d(g):
                decode(d_half[:, :, ds(g, 1), :, 0], 256, ("p (h o q) -> p h o q", dict(h=KT, o=1)),
                       d_code[:, :], d_step, d_codes, g)

            def lo_gu(g, m, piece):
                dve.wait_ge(w_hi_ok, piece + 1)
                cols = ds(g * D, D)
                lo_part(wgu_lo[:, m, :, cols], ps_w[:, :].rearrange("p (k n) -> p k n", k=KT),
                        wgu_hi[:, m, :, cols]).then_inc(w_lo_ok, 1)

            def lo_d(g, piece):
                dve.wait_ge(w_hi_ok, piece + 1)
                cols = ds(g * 2 * D, 2 * D)
                lo_part(wd_lo[:, cols], ps_w[:, :], wd_hi[:, cols]).then_inc(w_lo_ok, 1)

            def lo_h2(c, kt, psum):
                dve.wait_ge(h2_hi_ok, 2 * c + kt + 1)
                cols = slice(c * CHUNK, (c + 1) * CHUNK)
                lo_part(h2T_lo[:, kt, cols], psum[:, :], h2T_hi[:, kt, cols]).then_inc(h2_lo_ok, 1)

            def normalise_chunk(c):
                dve.wait_ge(rstd_ready, c + 3)
                for j in range(CT):
                    op = normalise(h2_sb[:, j, :].unsqueeze(1), CT * c + j)
                op.then_inc(h2_ready, 1)

            dve.wait_ge(s_x01, 16)
            ln_stats(0, 2)
            dve.wait_ge(s_tok, 16)
            ts(mask[:, 0, :], tok_sb[:, :], float(PER_EXPERT), None, ALU.is_lt).then_inc(ln_step, 1)
            ts(mask[:, 3, :], tok_sb[:, :], float(3 * PER_EXPERT), None, ALU.is_ge).then_inc(ln_step, 1)
            for k in range(2):
                ts(below[:, k, :], tok_sb[:, :], float((k + 2) * PER_EXPERT), None,
                   ALU.is_lt).then_inc(ln_step, 1)
            steps[0] += 4
            dve.wait_ge(ln_step, steps[0])
            for k in range(2):
                op = stt(mask[:, k + 1, :], tok_sb[:, :], float((k + 1) * PER_EXPERT), below[:, k, :],
                         ALU.is_ge, ALU.mult)
            op.then_inc(mask_ready, 1)
            dve.wait_ge(rstd_ready, 1)
            for j in range(2):
                normalise(h_sb[:, j, :].unsqueeze(1), j).then_inc(h_ready, 1)
            lo_h(0, 0)
            for half in range(2):
                for kt in range(KT):
                    dve.wait_ge(cT_hi_ok, 2 * half + kt + 1)
                    cols = slice(half * 512, half * 512 + 512)
                    lo_part(cT_lo[:, kt, cols], bank[2 * half + kt][:, :],
                            cT_hi[:, kt, cols]).then_inc(cT_lo_ok, 1)
            dve.wait_ge(s_x27, 16)
            ln_stats(2, TT - 2)
            gated(0)
            lo_h(1, 1)
            dve.wait_ge(s_gupk[0], 32)
            decode_gu(0)
            dve.wait_ge(rstd_ready, 2)

            with dve.Fori(0, TT // 2 - 1) as p:
                for u in range(2):
                    j = 2 * p + u
                    lo_a(j)
                    normalise(h_sb[:, u, :].unsqueeze(1), j + 2).then_inc(h_ready, 1)
                    gated(j + 1)
                    lo_h(j + 2, u)
                    residual1(j, u)
                    lo_gu(p, u, j)
                decode_gu(p + 1)
            lo_a(TT - 2)
            gated(TT - 1)
            dve.wait_ge(x1_ready, CT)
            ln_stats(0, CT)
            residual1(TT - 2, 0)
            normalise_chunk(0)
            lo_gu(HALF - 1, 0, piece_gu(HALF - 1, 0))
            lo_a(TT - 1)
            lo_h2(0, 0, ps_h)
            residual1(TT - 1, 1)
            lo_gu(HALF - 1, 1, piece_gu(HALF - 1, 1))
            lo_h2(0, 1, ps_h)
            dve.wait_ge(s_gupk[1], 32)
            decode_gu(HALF)
            dve.wait_ge(s_dpk, 16)
            decode_d(0)

            def multiply(n, u):
                dve.wait_ge(gelu_ready, n + 1)
                dve.wait_ge(up_ready, n + 1)
                tt(prod_sb[:, u, :], act_sb[:, u, :], ps_up[u][:, :], ALU.mult).then_inc(inter_ready, 1)

            def lo_inter(n, u):
                dve.wait_ge(i_hi_ok, n + 1)
                lo_part(prodT_lo[:, u, :], prod_sb[:, u, :], prodT_hi[:, u, :]).then_inc(i_lo_ok, 1)

            def chunk0_pair(t, early, next_gu, next_d=True, c1=False):
                multiply(2 * t, 0)
                lo_d(t, piece_d_early(t) if early else piece_d_late(t))
                lo_inter(2 * t, 0)
                if early:
                    lo_gu(t + HALF, 0, piece_gu_late(t, 0))
                if c1:
                    lo_h2(1, 0, ps_h)
                    lo_h2(1, 1, ps_w)
                multiply(2 * t + 1, 1)
                if early:
                    lo_gu(t + HALF, 1, piece_gu_late(t, 1))
                lo_inter(2 * t + 1, 1)
                if next_gu:
                    decode_gu(t + HALF + 1)
                if next_d:
                    decode_d(t + 1)

            with dve.Fori(0, HALF - 1) as t:
                chunk0_pair(t, True, True)
            chunk0_pair(HALF - 1, True, False)
            dve.wait_ge(x1_ready, TT)
            ln_stats(CT, CT)
            normalise_chunk(1)
            with dve.Fori(HALF, NPAIR - 1) as t:
                chunk0_pair(t, False, False)
            chunk0_pair(NPAIR - 1, False, False, next_d=False, c1=True)

            def residual2(c):
                for pair in range(2):
                    n = 2 * c + pair
                    tiles = slice(2 * n, 2 * n + 2)
                    dve.wait_ge(out_ps, n + 1)
                    tt(x_sb[:, tiles, :], x_sb[:, tiles, :],
                       ps_out[pair][:, :].rearrange("p (j h) -> p j h", j=2), ALU.add).then_inc(res_ready, 1)

            multiply(NT, 0)
            lo_inter(NT, 0)
            multiply(NT + 1, 1)
            residual2(0)
            lo_inter(NT + 1, 1)
            with dve.Fori(NPAIR + 1, 2 * NPAIR) as t:
                for u in range(2):
                    multiply(2 * t + u, u)
                    lo_inter(2 * t + u, u)
            residual2(1)


_IN = [("x", (TOKENS, D), "float32"), ("itok_BxS_13_99985", (TOKENS,), "int32"), ("ctx_2048", (EF, D), "float32"),
       ("L0_ffn_gate_W_packed", (N, D // 2), "int32"), ("L0_ffn_gate_scales", (N, D // BLOCK), "float32"),
       ("L0_ffn_up_W_packed", (N, D // 2), "int32"), ("L0_ffn_up_scales", (N, D // BLOCK), "float32"),
       ("L0_ffn_down_W_packed", (D, N // 2), "int32"), ("L0_ffn_down_scales", (D, N // BLOCK), "float32")]


def kernel(**inputs):
    import numpy as np
    import concourse.bacc as bacc
    from concourse.bass_utils import run_bass_kernel_spmd

    nc = bacc.Bacc("TRN2", target_bir_lowering=False, num_devices=1)
    arrays, args = {}, []
    for name, shape, dtype in _IN:
        a = np.ascontiguousarray(inputs[name]).reshape(shape)
        arrays[f"in_{name}"] = a
        args.append(nc.dram_tensor(f"in_{name}", a.shape, mybir.dt.from_np(a.dtype), kind="ExternalInput").ap())
    args.append(nc.dram_tensor("out_x", (TOKENS, D), mybir.dt.float32, kind="ExternalOutput").ap())
    xattn_ffn(nc, *args)
    result = run_bass_kernel_spmd(nc, [arrays], core_ids=[0])
    return result.results[0]["out_x"].reshape(4, 256, 256)
```

```python
import concourse.bass as bass
from concourse import mybir
from contextlib import ExitStack

P = 128
TOKENS, D = 1024, 256
TT = TOKENS // P
KT = D // P
CHUNK = 512
CT = CHUNK // P
E = 4
EF = E * 256
QI = E * KT
EI = 2 * QI
PER_EXPERT = 12500 // E
EPS = 1e-5
N = 2048
NT = N // P
NPAIR = NT // 2
BLOCK = 32
FP4_SHIFT = 64.0

EARLY = 2
LATE = NPAIR - EARLY
H_AT = {5: 2, 6: 3, 14: 4, 15: 5}
W_AT = {7: 0, 8: 1, 12: 2, 13: 3}
STATS_AT = {1: (1, 0), 2: (1, 1), 10: (2, 0), 11: (2, 1)}
NORM_AT = {3: (1, 0), 4: (1, 1), 12: (2, 0), 13: (2, 1)}
DECODE_AT = {5: 0, 9: 1}


def xattn_ffn(nc, x, tok, ctx_w, gate_w, gate_s, up_w, up_s, down_w, down_s, out):
    fp32, f32r, bf16 = mybir.dt.float32, mybir.dt.float32r, mybir.dt.bfloat16
    i32, u16, fp8 = mybir.dt.int32, mybir.dt.uint16, mybir.dt.float8e4
    ALU, ACT = mybir.AluOpType, mybir.ActivationFunctionType
    ds = bass.ds

    stack = ExitStack()
    with stack:
        def sb(name, shape, dt):
            return stack.enter_context(nc.sbuf_tensor(name, shape, dt))

        def sem(name):
            return stack.enter_context(nc.semaphore(name))

        x_sb = sb("x_sb", [P, TT, D], fp32)
        pick = sb("pick", [TT, TT, P], bf16)
        ident = sb("ident", [P, P], fp32)
        neg_half = sb("neg_half", [P, TT], fp32)
        warm = sb("warm", [1, 2], fp32)
        stats = sb("stats", [P, TT, 6], fp32)
        mean_var = sb("mean_var", [P, TT, 2], fp32)
        var = sb("var", [P, TT], fp32)
        rstd = sb("rstd", [P, TT], fp32)
        ctx_sb = sb("ctx_sb", [P, TT * D], fp32)
        def all_masks(words):
            return words.bitcast(bf16).rearrange("p (j e t) -> p j e t", j=CT, e=E)
        d_pk = sb("d_pk", [P, KT * N // 2], i32)
        words = CT * E * P // 2
        small = d_pk[0:TT, words:]
        tok_sb = small[:, 0:P]
        below = small[:, P:3 * P].bitcast(fp32).rearrange("j (k t) -> j k t", k=2)
        mask_row = small[:, 3 * P:5 * P].bitcast(bf16).rearrange("j (e t) -> j e t", e=E)
        mask = (all_masks(d_pk[:, 0:words]), all_masks(ctx_sb[:, 0:words]))
        outT_sb = ctx_sb[:, 0:KT * CHUNK].rearrange("p (h t) -> p h t", h=KT)
        h_sb = sb("h_sb", [P, CT, D], fp32)
        cT_hi = sb("cT_hi", [P, KT, EF], f32r)
        cT_lo = sb("cT_lo", [P, KT, EF], f32r)
        hT_hi = sb("hT_hi", [P, KT, TOKENS], f32r)
        hT_lo = sb("hT_lo", [P, KT, TOKENS], f32r)
        act_sb = sb("act_sb", [P, 2, CHUNK], fp32)
        prod_sb = sb("prod_sb", [P, 2, CHUNK], fp32)
        prod_hi = sb("prod_hi", [P, 2, CHUNK], f32r)
        prod_lo = sb("prod_lo", [P, 2, CHUNK], f32r)
        gu_pk = sb("gu_pk", [P, 2, NT * 128], i32)
        gu_sc = sb("gu_sc", [P, 2, NPAIR, 16], fp32)
        d_sc = sb("d_sc", [P, KT * N // BLOCK], fp32)
        d_scx = sb("d_scx", [P, KT, 128], fp32)
        code_hi = sb("code_hi", [P, 512], u16)
        code_lh = sb("code_lh", [P, 512], u16)
        code_mag = sb("code_mag", [P, 512], u16)
        code_sgn = sb("code_sgn", [P, 512], u16)
        gu_code = sb("gu_code", [P, 512], u16)
        d_code = sb("d_code", [P, 256], u16)
        gu_nat = sb("gu_nat", [P, 2, 2, D], fp32)
        d_nat = sb("d_nat", [P, KT, 2, P], fp32)
        wgu_hi = sb("wgu_hi", [P, 2, KT, N], f32r)
        wgu_lo = sb("wgu_lo", [P, 2, KT, N], f32r)
        wd_hi = sb("wd_hi", [P, NT * D], f32r)
        wd_lo = sb("wd_lo", [P, NT * D], f32r)

        bank = [stack.enter_context(nc.psum_tensor(f"bank{b}", [P, 512], fp32)) for b in range(8)]
        ps_z = bank[0:2]
        ps_y = (bank[4:6], bank[2:4])
        ps_gate, ps_up, ps_o = (bank[0], bank[2]), (bank[1], bank[3]), bank[4:6]
        ps_h, ps_w = bank[6], bank[7]
        ps_out = (bank[6], bank[7])

        s_tok = sem("s_tok")
        s_x, s_ctx = [sem("s_x0"), sem("s_x1"), sem("s_x2")], [sem("s_ctx0"), sem("s_ctx1")]
        s_gusc, s_dsc = sem("s_gusc"), sem("s_dsc")
        s_gupk, s_dpk = [sem("s_gupk0"), sem("s_gupk1")], sem("s_dpk")
        s_out = [sem(f"s_out{n}") for n in range(4)]
        pick_ok, ident_ok, pow_ok = sem("pick_ok"), sem("ident_ok"), sem("pow_ok")
        scales_ok = sem("scales_ok")
        mask_step, mask_rows = sem("mask_step"), sem("mask_rows")
        mask_ps, mask_ok = sem("mask_ps"), sem("mask_ok")
        ln_step = sem("ln_step")
        var_ready = sem("var_ready")
        rstd_ready = sem("rstd_ready")
        cT_ps, cT_hi_ok, cT_lo_ok = sem("cT_ps"), sem("cT_hi_ok"), sem("cT_lo_ok")
        h_ready = sem("h_ready")
        h_ps, h_hi_ok, h_lo_ok = sem("h_ps"), sem("h_hi_ok"), sem("h_lo_ok")
        z_ready = sem("z_ready")
        silu_ready = sem("silu_ready")
        a_ready = sem("a_ready")
        am_ready = sem("am_ready")
        a_hi_ok, a_lo_ok = sem("a_hi_ok"), sem("a_lo_ok")
        y_done = sem("y_done")
        x1_ready = sem("x1_ready")
        gu_step, d_step = sem("gu_step"), sem("d_step")
        gu_codes, d_codes = sem("gu_codes"), sem("d_codes")
        gu_nat_ok, d_nat_ok = sem("gu_nat_ok"), sem("d_nat_ok")
        w_ps, w_hi_ok, w_lo_ok = sem("w_ps"), sem("w_hi_ok"), sem("w_lo_ok")
        gate_ready, up_ready = sem("gate_ready"), sem("up_ready")
        gelu_ready = sem("gelu_ready")
        inter_ready = sem("inter_ready")
        i_hi_ok, i_lo_ok = sem("i_hi_ok"), sem("i_lo_ok")
        o_ready = sem("o_ready")
        outT_ok = sem("outT_ok")
        out_ps = sem("out_ps")
        res_ready = sem("res_ready")

        def piece_gu_late(t, m):
            return 2 * EARLY + 3 * t + 1 + m

        def piece_d_early(t):
            return 2 * EARLY + 3 * t

        def piece_d_late(t):
            return 2 * EARLY + 2 * LATE + t

        def piece_d(t):
            return piece_d_early(t) if t < LATE else piece_d_late(t)

        x_v = x.rearrange("(j p) d -> p j d", p=P)
        out_v = out.rearrange("(j p) d -> p j d", p=P)
        chunk_cols = [slice(c * CHUNK, (c + 1) * CHUNK) for c in range(2)]
        block = stack.enter_context(nc.Block())

        @block.sync
        def _(sp):
            ctx_v = ctx_w.rearrange("(b p) c -> p b c", p=P)
            ctx_blocks = ctx_sb[:, :].rearrange("p (b c) -> p b c", b=TT)
            sp.dma_start(tok_sb[:, :], tok.rearrange("(j p) -> j p", p=P)).then_inc(s_tok, 16)
            for half in range(2):
                tiles = slice(2 * half, 2 * half + 2)
                sp.dma_start(x_sb[:, tiles, :], x_v[:, tiles, :]).then_inc(s_x[half], 16)
            for half in range(2):
                blocks = slice(CT * half, CT * half + CT)
                sp.dma_start(ctx_blocks[:, blocks, :], ctx_v[:, blocks, :]).then_inc(s_ctx[half], 16)
            sp.dma_start(x_sb[:, CT:TT, :], x_v[:, CT:TT, :]).then_inc(s_x[2], 16)
            for m, s in enumerate((gate_s, up_s)):
                sp.dma_start(gu_sc[:, m, :, :],
                             s.rearrange("(p g i) b -> p g (i b)", g=NPAIR, i=2)).then_inc(s_gusc, 16)
            sp.dma_start(d_sc[:, :].rearrange("p (h b) -> p h b", h=KT),
                         down_s.rearrange("(h p) b -> p h b", p=P)).then_inc(s_dsc, 16)
            for part in range(2):
                cols = slice(part * N // 2, (part + 1) * N // 2)
                for m, w in enumerate((gate_w, up_w)):
                    sp.dma_start(gu_pk[:, m, cols],
                                 w.rearrange("(p i) c -> p (i c)", i=NT)[:, cols]).then_inc(s_gupk[part], 16)
            sp.wait_ge(mask_ok, TT)
            sp.wait_ge(am_ready, QI)
            sp.dma_start(d_pk[:, :].rearrange("p (h c) -> p h c", h=KT),
                         down_w.rearrange("(h p) c -> p h c", p=P)).then_inc(s_dpk, 16)
            for n in range(4):
                sp.wait_ge(res_ready, n + 1)
                sp.dma_start(out_v[:, 2 * n:2 * n + 2, :], x_sb[:, 2 * n:2 * n + 2, :]).then_inc(s_out[n], 16)
            for n in range(4):
                sp.wait_ge(s_out[n], 16)

        @block.gpsimd
        def _(pool):
            nc.gpsimd.memset(pick[:, :, :], 0.0).then_inc(pick_ok, 1)
            nc.gpsimd.memset(ident[:, :], 0.0).then_inc(ident_ok, 1)
            nc.gpsimd.memset(neg_half[:, :], -0.5).then_inc(pow_ok, 1)
            pool.wait_ge(pick_ok, 1)
            nc.gpsimd.affine_select(out=pick[:, :, :], in_=pick[:, :, :], compare_op=ALU.not_equal, fill=1.0,
                                    base=0, pattern=[[-1, TT], [0, P]], channel_multiplier=1).then_inc(pick_ok, 1)
            pool.wait_ge(ident_ok, 1)
            nc.gpsimd.affine_select(out=ident[:, :], in_=ident[:, :], compare_op=ALU.not_equal, fill=1.0,
                                    base=0, pattern=[[-1, P]], channel_multiplier=1).then_inc(ident_ok, 1)
            pool.wait_ge(pow_ok, 1)

            def inv_std(batch):
                pool.wait_ge(var_ready, batch + 1)
                t = slice(CT * (batch % 2), CT * (batch % 2) + CT)
                nc.gpsimd.tensor_tensor(rstd[:, t], var[:, t], neg_half[:, t], ALU.pow).then_inc(rstd_ready, 1)

            def masked(n):
                c, e = n // QI, n % QI // KT
                pool.wait_ge(a_ready, n + 1)
                if n % QI == 0:
                    pool.wait_ge(mask_ok, CT * (c + 1))
                item = prod_sb[:, n % 2, :].rearrange("p (j t) -> p j t", j=CT)
                nc.gpsimd.tensor_tensor(item, item, mask[c][:, :, e, :],
                                        ALU.mult).then_inc(am_ready, 1)

            def dequant_gu(g):
                pool.wait_ge(gu_codes, g + 1)
                for m in range(2):
                    nc.gpsimd.tensor_tensor(
                        gu_nat[:, m, :, :].rearrange("p i (b c) -> p (i b) c", c=BLOCK),
                        gu_code[:, 256 * m:256 * (m + 1)].bitcast(fp8).rearrange("p (b c) -> p b c", c=BLOCK),
                        gu_sc[:, m, g, :].unsqueeze(2).to_broadcast([P, 16, BLOCK]),
                        ALU.mult).then_inc(gu_nat_ok, 1)

            def dequant_d(g):
                pool.wait_ge(d_codes, g + 1)
                nc.gpsimd.tensor_tensor(
                    d_nat[:, :, :, :].rearrange("p h i q -> p h q i"),
                    d_code[:, :].bitcast(fp8).rearrange("p (h q i) -> p h q i", h=KT, i=2),
                    d_scx[:, :, :].unsqueeze(3).to_broadcast([P, KT, P, 2]),
                    ALU.mult).then_inc(d_nat_ok, 1)

            def lo_inter(n, u):
                pool.wait_ge(i_hi_ok, n + 1)
                nc.gpsimd.tensor_tensor(prod_lo[:, u, :], prod_sb[:, u, :], prod_hi[:, u, :].bitcast(fp32),
                                        ALU.subtract).then_inc(i_lo_ok, 1)

            inv_std(0)
            masked(0)
            masked(1)
            masked(2)
            inv_std(1)
            pool.wait_ge(s_gusc, 32)
            nc.gpsimd.tensor_scalar(gu_sc[:, :, :, :].rearrange("p m g b -> p (m g b)"),
                                    gu_sc[:, :, :, :].rearrange("p m g b -> p (m g b)"),
                                    FP4_SHIFT, 1.0, ALU.mult, ALU.mult).then_inc(scales_ok, 1)
            pool.wait_ge(s_dsc, 16)
            nc.gpsimd.tensor_scalar(d_scx[:, :, :].rearrange("p h (b s) -> p (h b) s", s=2),
                                    d_sc[:, :].unsqueeze(2).to_broadcast([P, KT * N // BLOCK, 2]),
                                    FP4_SHIFT, 1.0, ALU.mult, ALU.mult).then_inc(scales_ok, 1)
            pool.wait_ge(scales_ok, 2)
            for n in range(3, EI):
                masked(n)
                if n in DECODE_AT:
                    dequant_gu(DECODE_AT[n])
                if n == 11:
                    inv_std(2)
            dequant_d(0)
            for t in range(NPAIR):
                if t < LATE:
                    dequant_gu(t + EARLY)
                lo_inter(2 * t, 0)
                if t + 1 < NPAIR:
                    dequant_d(t + 1)
                lo_inter(2 * t + 1, 1)
                if t == 1:
                    inv_std(3)
            with pool.Fori(NPAIR, 2 * NPAIR) as t:
                for u in range(2):
                    lo_inter(2 * t + u, u)

        def products(psum, terms, first=True, last=True):
            n = 0
            for w_hi, w_lo, m_hi, m_lo in terms:
                for w, m in ((w_hi, m_hi), (w_hi, m_lo), (w_lo, m_hi)):
                    mm = nc.tensor.matmul(psum, w, m, start=first and n == 0,
                                          stop=last and n == 3 * len(terms) - 1, skip_group_check=True)
                    n += 1
            return mm

        @block.tensor
        def _(pe):
            def spread_mask(j):
                if j >= 2:
                    pe.wait_ge(mask_ok, j - 1)
                nc.tensor.matmul(bank[4 + j % 2][:, :], pick[:, j, :], mask_row[:, :, :],
                                 start=True, stop=True).then_inc(mask_ps, 1)

            def transpose_h(piece, psum, taken=None):
                pe.wait_ge(h_ready, CT * (piece // 2 + 1))
                if taken is not None:
                    pe.wait_ge(h_lo_ok, taken)
                for j in range(CT):
                    mm = nc.tensor.transpose(psum[:, j * P:(j + 1) * P],
                                             h_sb[:, j, piece % 2 * P:(piece % 2 + 1) * P], ident[:, :])
                mm.then_inc(h_ps, 1)

            def transpose_gu(g, m, piece):
                if piece:
                    pe.wait_ge(w_lo_ok, piece)
                pe.wait_ge(gu_nat_ok, 2 * g + m + 1)
                for kt in range(KT):
                    for i in range(2):
                        c = (2 * kt + i) * P
                        mm = nc.tensor.transpose(ps_w[:, c:c + P], gu_nat[:, m, i, kt * P:(kt + 1) * P],
                                                 ident[:, :])
                mm.then_inc(w_ps, 1)

            def transpose_d(g, piece):
                pe.wait_ge(w_lo_ok, piece)
                pe.wait_ge(d_nat_ok, g + 1)
                for i in range(2):
                    for hb in range(KT):
                        c = (2 * i + hb) * P
                        mm = nc.tensor.transpose(ps_w[:, c:c + P], d_nat[:, hb, i, :], ident[:, :])
                mm.then_inc(w_ps, 1)

            def expert_in(n):
                c, q = n // QI, n % QI
                if n >= 2:
                    pe.wait_ge(a_ready, n - 1)
                for kt in range(KT):
                    if q == 0:
                        pe.wait_ge(h_lo_ok, 2 * c + kt + 1)
                    mm = products(ps_z[n % 2][:, :],
                                  [(cT_hi[:, kt, q * P:(q + 1) * P], cT_lo[:, kt, q * P:(q + 1) * P],
                                    hT_hi[:, kt, chunk_cols[c]], hT_lo[:, kt, chunk_cols[c]])],
                                  first=kt == 0, last=kt == KT - 1)
                mm.then_inc(z_ready, 1)

            def expert_out(n):
                c, e, f = n // QI, n % QI // KT, n % KT
                pe.wait_ge(a_lo_ok, n + 1)
                for j in range(CT):
                    cols = slice(j * P, (j + 1) * P)
                    mm = products(ps_y[c][j // 2][:, j % 2 * D:(j % 2 + 1) * D],
                                  [(prod_hi[:, n % 2, cols], prod_lo[:, n % 2, cols],
                                    cT_hi[:, f, e * D:(e + 1) * D], cT_lo[:, f, e * D:(e + 1) * D])],
                                  first=n % QI == 0 and j % 2 == 0, last=n % QI == QI - 1)
                mm.then_inc(y_done, 1)

            def gate_up(n):
                c, i = n // NT, n % NT
                for m, (psum, ready) in enumerate(((ps_gate, gate_ready), (ps_up, up_ready))):
                    products(psum[n % 2][:, :],
                             [(wgu_hi[:, m, kt, i * P:(i + 1) * P], wgu_lo[:, m, kt, i * P:(i + 1) * P],
                               hT_hi[:, kt, chunk_cols[c]], hT_lo[:, kt, chunk_cols[c]]) for kt in range(KT)]
                             ).then_inc(ready, 1)

            def down(n):
                i, u = n % NT, n % 2
                w = [slice(i * D + hb * P, i * D + (hb + 1) * P) for hb in range(KT)]
                pe.wait_ge(i_hi_ok, n + 1)
                for hb in range(KT):
                    nc.tensor.matmul(ps_o[hb][:, :], wd_hi[:, w[hb]], prod_hi[:, u, :], start=i == 0, stop=False)
                    nc.tensor.matmul(ps_o[hb][:, :], wd_lo[:, w[hb]], prod_hi[:, u, :], start=False, stop=False)
                pe.wait_ge(i_lo_ok, n + 1)
                for hb in range(KT):
                    mm = nc.tensor.matmul(ps_o[hb][:, :], wd_hi[:, w[hb]], prod_lo[:, u, :], start=False,
                                          stop=i == NT - 1)
                    if i == NT - 1:
                        mm.then_inc(o_ready, 1)

            def transpose_out(c):
                pe.wait_ge(outT_ok, KT * (c + 1))
                for pair in range(2):
                    for j in range(2):
                        for hb in range(KT):
                            t = (2 * pair + j) * P
                            mm = nc.tensor.transpose(ps_out[pair][:, (2 * j + hb) * P:(2 * j + hb + 1) * P],
                                                     outT_sb[:, hb, t:t + P], ident[:, :])
                    mm.then_inc(out_ps, 1)

            pe.wait_ge(pick_ok, 2)
            pe.wait_ge(mask_rows, 1)
            for j in range(CT):
                spread_mask(j)
            pe.wait_ge(ident_ok, 2)
            for half in range(2):
                pe.wait_ge(s_ctx[half], 16)
                for kt in range(KT):
                    for b in range(4):
                        r = (4 * half + b) * D + kt * P
                        mm = nc.tensor.transpose(bank[2 * half + kt][:, b * P:(b + 1) * P],
                                                 ctx_sb[:, r:r + P], ident[:, :])
                    mm.then_inc(cT_ps, 1)
                if half == 0:
                    for j in range(CT):
                        pe.wait_ge(h_ready, j + 1)
                        for kt, psum in enumerate((ps_h, ps_w)):
                            mm = nc.tensor.transpose(psum[:, j * P:(j + 1) * P],
                                                     h_sb[:, j, kt * P:(kt + 1) * P], ident[:, :])
                            if j == CT - 1:
                                mm.then_inc(h_ps, 1)
            pe.wait_ge(cT_lo_ok, 2)
            expert_in(0)
            spread_mask(CT)
            spread_mask(CT + 1)
            expert_in(1)
            spread_mask(CT + 2)
            spread_mask(CT + 3)
            for n in range(2, EI):
                if n == QI // 2:
                    pe.wait_ge(cT_lo_ok, 4)
                expert_in(n)
                if n == 2:
                    pe.wait_ge(mask_ok, TT)
                expert_out(n - 2)
                if n in H_AT:
                    transpose_h(H_AT[n], ps_h, taken=H_AT[n])
                if n in W_AT:
                    transpose_gu(W_AT[n] // 2, W_AT[n] % 2, W_AT[n])
            expert_out(EI - 2)
            pe.wait_ge(h_lo_ok, 6)
            pe.wait_ge(w_lo_ok, 2)
            pe.wait_ge(a_ready, EI)
            for t in range(NPAIR):
                if t > 0:
                    pe.wait_ge(w_lo_ok, 2 * (t + 1) if t < EARLY else piece_gu_late(t - EARLY, 1) + 1)
                gate_up(2 * t)
                if t == 0:
                    expert_out(EI - 1)
                transpose_d(t, piece_d(t))
                if t > 0:
                    down(2 * t - 1)
                if t == 0:
                    pe.wait_ge(x1_ready, 4)
                if t == NPAIR - 1:
                    transpose_h(6, ps_h)
                    pe.wait_ge(w_lo_ok, piece_d(t) + 1)
                    transpose_h(7, ps_w)
                gate_up(2 * t + 1)
                if t < LATE:
                    transpose_gu(t + EARLY, 0, piece_gu_late(t, 0))
                else:
                    pe.wait_ge(w_lo_ok, piece_d(t) + 1)
                down(2 * t)
                if t < LATE:
                    transpose_gu(t + EARLY, 1, piece_gu_late(t, 1))
            pe.wait_ge(h_lo_ok, 8)
            for n in range(NT, 2 * NT):
                gate_up(n)
                if n == NT + 1:
                    transpose_out(0)
                down(n - 1)
            down(2 * NT - 1)
            transpose_out(1)

        @block.scalar
        def _(act):
            def hi_part(dst, src):
                return nc.scalar.activation(dst, src, ACT.Copy)

            def take_mask(j):
                act.wait_ge(mask_ps, j + 1)
                nc.scalar.copy(mask[j // CT][:, j % CT, :, :].rearrange("p e t -> p (e t)"),
                               bank[4 + j % 2][:, :]).then_inc(mask_ok, 1)

            def hi_h(piece, psum):
                act.wait_ge(h_ps, piece + 1)
                hi_part(hT_hi[:, piece % 2, chunk_cols[piece // 2 % 2]], psum[:, :]).then_inc(h_hi_ok, 1)

            def silu(n):
                act.wait_ge(z_ready, n + 1)
                nc.scalar.activation(act_sb[:, n % 2, :], ps_z[n % 2][:, :], ACT.Silu).then_inc(silu_ready, 1)

            def hi_a(n):
                act.wait_ge(am_ready, n + 1)
                if n >= 2:
                    act.wait_ge(y_done, n - 1)
                hi_part(prod_hi[:, n % 2, :], prod_sb[:, n % 2, :]).then_inc(a_hi_ok, 1)

            def hi_gu(g, m, piece):
                act.wait_ge(w_ps, piece + 1)
                hi_part(wgu_hi[:, m, :, ds(g * D, D)],
                        ps_w[:, :].rearrange("p (k n) -> p k n", k=KT)).then_inc(w_hi_ok, 1)

            def hi_d(g, piece):
                act.wait_ge(w_ps, piece + 1)
                hi_part(wd_hi[:, ds(g * 2 * D, 2 * D)], ps_w[:, :]).then_inc(w_hi_ok, 1)

            def gelu(n, u):
                act.wait_ge(gate_ready, n + 1)
                nc.scalar.activation(act_sb[:, u, :], ps_gate[u][:, :],
                                     ACT.Gelu_apprx_tanh).then_inc(gelu_ready, 1)

            def hi_inter(n, u):
                act.wait_ge(inter_ready, n + 1)
                hi_part(prod_hi[:, u, :], prod_sb[:, u, :]).then_inc(i_hi_ok, 1)

            def take_out(c):
                act.wait_ge(o_ready, KT * c + 1)
                nc.scalar.copy(outT_sb[:, 0, :], ps_o[0][:, :]).then_inc(outT_ok, 1)

            act.wait_ge(pow_ok, 1)
            nc.scalar.activation(warm[:, 0:1], neg_half[0:1, 0:1], ACT.Silu)
            for j in range(CT):
                take_mask(j)
            for half in range(2):
                for kt in range(KT):
                    act.wait_ge(cT_ps, 2 * half + kt + 1)
                    hi_part(cT_hi[:, kt, half * 512:half * 512 + 512],
                            bank[2 * half + kt][:, :]).then_inc(cT_hi_ok, 1)
                if half == 0:
                    hi_h(0, ps_h)
                    hi_h(1, ps_w)
            silu(0)
            take_mask(CT)
            take_mask(CT + 1)
            silu(1)
            hi_a(0)
            take_mask(CT + 2)
            take_mask(CT + 3)
            for n in range(2, EI):
                silu(n)
                hi_a(n - 1)
                if n in H_AT:
                    hi_h(H_AT[n], ps_h)
                if n in W_AT:
                    hi_gu(W_AT[n] // 2, W_AT[n] % 2, W_AT[n])
            hi_a(EI - 1)
            nc.scalar.activation(warm[:, 1:2], neg_half[0:1, 0:1], ACT.Gelu_apprx_tanh)

            def chunk0_pair(t, early, last=False):
                gelu(2 * t, 0)
                hi_d(t, piece_d_early(t) if early else piece_d_late(t))
                hi_inter(2 * t, 0)
                if last:
                    hi_h(6, ps_h)
                    hi_h(7, ps_w)
                gelu(2 * t + 1, 1)
                if early:
                    hi_gu(t + EARLY, 0, piece_gu_late(t, 0))
                hi_inter(2 * t + 1, 1)
                if early:
                    hi_gu(t + EARLY, 1, piece_gu_late(t, 1))

            with act.Fori(0, LATE) as t:
                chunk0_pair(t, True)
            with act.Fori(LATE, NPAIR - 1) as t:
                chunk0_pair(t, False)
            chunk0_pair(NPAIR - 1, False, last=True)

            gelu(NT, 0)
            hi_inter(NT, 0)
            take_out(0)
            gelu(NT + 1, 1)
            hi_inter(NT + 1, 1)
            with act.Fori(NPAIR + 1, 2 * NPAIR) as t:
                for u in range(2):
                    gelu(2 * t + u, u)
                    hi_inter(2 * t + u, u)
            take_out(1)

        @block.vector
        def _(dve):
            tt, ts, stt = nc.vector.tensor_tensor, nc.vector.tensor_scalar, nc.vector.scalar_tensor_tensor

            def lo_part(dst, src, hi):
                return tt(dst, src, hi.bitcast(fp32), ALU.subtract)

            def ln_stats(batch, half):
                t0, base = CT * (batch % 2), 8 * batch
                for j in range(t0 + 2 * half, t0 + 2 * half + 2):
                    nc.vector.bn_stats(stats[:, j, :], x_sb[:, j, :]).then_inc(ln_step, 1)
                dve.wait_ge(ln_step, base + 4 * half + 2)
                for j in range(t0 + 2 * half, t0 + 2 * half + 2):
                    nc.vector.bn_aggr(mean_var[:, j, :], stats[:, j, :]).then_inc(ln_step, 1)
                if half == 1:
                    dve.wait_ge(ln_step, base + 8)
                    ts(var[:, t0:t0 + CT], mean_var[:, t0:t0 + CT, 1], EPS, None, ALU.add).then_inc(var_ready, 1)

            def normalise(batch, half):
                dve.wait_ge(rstd_ready, batch + 1)
                for k in (2 * half, 2 * half + 1):
                    j = CT * (batch % 2) + k
                    ts(h_sb[:, k, :], x_sb[:, j, :], mean_var[:, j, 0:1], rstd[:, j:j + 1],
                       ALU.subtract, ALU.mult).then_inc(h_ready, 1)

            def lo_h(piece, psum):
                dve.wait_ge(h_hi_ok, piece + 1)
                kt, cols = piece % 2, chunk_cols[piece // 2 % 2]
                lo_part(hT_lo[:, kt, cols], psum[:, :], hT_hi[:, kt, cols]).then_inc(h_lo_ok, 1)

            def gated(n):
                if n >= 2:
                    dve.wait_ge(a_lo_ok, n - 1)
                dve.wait_ge(silu_ready, n + 1)
                tt(prod_sb[:, n % 2, :], act_sb[:, n % 2, :], ps_z[n % 2][:, :], ALU.mult).then_inc(a_ready, 1)

            def lo_a(n):
                dve.wait_ge(a_hi_ok, n + 1)
                lo_part(prod_lo[:, n % 2, :], prod_sb[:, n % 2, :], prod_hi[:, n % 2, :]).then_inc(a_lo_ok, 1)

            def residual1(c, pair):
                dve.wait_ge(y_done, QI * (c + 1))
                tiles = slice(CT * c + 2 * pair, CT * c + 2 * pair + 2)
                tt(x_sb[:, tiles, :], x_sb[:, tiles, :],
                   ps_y[c][pair][:, :].rearrange("p (j d) -> p j d", j=2), ALU.add).then_inc(x1_ready, 1)

            def decode(pk, n, shape, out_code, step, done, g):
                def v(tensor):
                    return tensor[:, 0:n].rearrange(shape[0], **shape[1])
                nib_hi, nib = v(code_hi), v(code_lh)
                shl, land, lor = ALU.logical_shift_left, ALU.bitwise_and, ALU.bitwise_or
                ts(nib_hi, pk, 4, 0x0f00, shl, land).then_inc(step, 1)
                dve.wait_ge(step, 4 * g + 1)
                stt(nib, pk, 0x000f, nib_hi, land, lor).then_inc(step, 1)
                dve.wait_ge(step, 4 * g + 2)
                ts(code_mag[:, 0:n], code_lh[:, 0:n], 2, 0x1c1c, shl, land).then_inc(step, 1)
                ts(code_sgn[:, 0:n], code_lh[:, 0:n], 4, 0x8080, shl, land).then_inc(step, 1)
                dve.wait_ge(step, 4 * g + 4)
                tt(out_code, code_mag[:, 0:n], code_sgn[:, 0:n], lor).then_inc(done, 1)

            gu_half = gu_pk[:, :, :].bitcast(u16).rearrange("p m (g c two) -> p m g c two", g=NPAIR, two=2)
            d_half = d_pk[:, :].bitcast(u16).rearrange("p (h q g two) -> p h g q two", h=KT, g=NPAIR, two=2)

            def decode_gu(g):
                decode(gu_half[:, :, ds(g, 1), :, 0], 512, ("p (m o c) -> p m o c", dict(m=2, o=1)),
                       gu_code[:, :], gu_step, gu_codes, g)

            def decode_d(g):
                decode(d_half[:, :, ds(g, 1), :, 0], 256, ("p (h o q) -> p h o q", dict(h=KT, o=1)),
                       d_code[:, :], d_step, d_codes, g)

            def lo_gu(g, m, piece):
                dve.wait_ge(w_hi_ok, piece + 1)
                cols = ds(g * D, D)
                lo_part(wgu_lo[:, m, :, cols], ps_w[:, :].rearrange("p (k n) -> p k n", k=KT),
                        wgu_hi[:, m, :, cols]).then_inc(w_lo_ok, 1)

            def lo_d(g, piece):
                dve.wait_ge(w_hi_ok, piece + 1)
                cols = ds(g * 2 * D, 2 * D)
                lo_part(wd_lo[:, cols], ps_w[:, :], wd_hi[:, cols]).then_inc(w_lo_ok, 1)

            dve.wait_ge(s_tok, 16)
            for k in range(2):
                ts(below[:, k, :], tok_sb[:, :], float((k + 2) * PER_EXPERT), None,
                   ALU.is_lt).then_inc(mask_step, 1)
            ts(mask_row[:, 0, :], tok_sb[:, :], float(PER_EXPERT), None, ALU.is_lt)
            ts(mask_row[:, 3, :], tok_sb[:, :], float(3 * PER_EXPERT), None, ALU.is_ge)
            dve.wait_ge(mask_step, 2)
            for k in range(2):
                op = stt(mask_row[:, k + 1, :], tok_sb[:, :], float((k + 1) * PER_EXPERT), below[:, k, :],
                         ALU.is_ge, ALU.mult)
            op.then_inc(mask_rows, 1)
            for half in range(2):
                dve.wait_ge(s_x[half], 16)
                ln_stats(0, half)
            normalise(0, 0)
            normalise(0, 1)
            for half in range(2):
                for kt in range(KT):
                    dve.wait_ge(cT_hi_ok, 2 * half + kt + 1)
                    cols = slice(half * 512, half * 512 + 512)
                    lo_part(cT_lo[:, kt, cols], bank[2 * half + kt][:, :],
                            cT_hi[:, kt, cols]).then_inc(cT_lo_ok, 1)
                if half == 0:
                    lo_h(0, ps_h)
                    lo_h(1, ps_w)

            gated(0)
            dve.wait_ge(s_x[2], 16)
            dve.wait_ge(s_gupk[0], 32)
            for n in range(1, EI):
                gated(n)
                lo_a(n - 1)
                if n in H_AT:
                    lo_h(H_AT[n], ps_h)
                if n in W_AT:
                    lo_gu(W_AT[n] // 2, W_AT[n] % 2, W_AT[n])
                if n in DECODE_AT:
                    decode_gu(DECODE_AT[n])
                if n in (9, 10):
                    residual1(0, n - 9)
                if n == 10:
                    dve.wait_ge(x1_ready, 2)
                if n in STATS_AT:
                    ln_stats(*STATS_AT[n])
                if n in NORM_AT:
                    normalise(*NORM_AT[n])
            dve.wait_ge(s_dpk, 16)
            decode_d(0)
            lo_a(EI - 1)
            dve.wait_ge(s_gupk[1], 32)

            def multiply(n, u):
                dve.wait_ge(gelu_ready, n + 1)
                dve.wait_ge(up_ready, n + 1)
                tt(prod_sb[:, u, :], act_sb[:, u, :], ps_up[u][:, :], ALU.mult).then_inc(inter_ready, 1)

            def chunk0_pair(t, early, first=False, last=False):
                if early:
                    decode_gu(t + EARLY)
                multiply(2 * t, 0)
                if first:
                    residual1(1, 0)
                    residual1(1, 1)
                lo_d(t, piece_d_early(t) if early else piece_d_late(t))
                if not last:
                    decode_d(t + 1)
                else:
                    lo_h(6, ps_h)
                    lo_h(7, ps_w)
                multiply(2 * t + 1, 1)
                if early:
                    lo_gu(t + EARLY, 0, piece_gu_late(t, 0))
                    lo_gu(t + EARLY, 1, piece_gu_late(t, 1))

            chunk0_pair(0, True, first=True)
            chunk0_pair(1, True)
            dve.wait_ge(x1_ready, 4)
            ln_stats(3, 0)
            ln_stats(3, 1)
            chunk0_pair(2, True)
            normalise(3, 0)
            normalise(3, 1)
            with dve.Fori(3, LATE) as t:
                chunk0_pair(t, True)
            with dve.Fori(LATE, NPAIR - 1) as t:
                chunk0_pair(t, False)
            chunk0_pair(NPAIR - 1, False, last=True)

            def take_out(c):
                dve.wait_ge(o_ready, KT * c + 2)
                nc.vector.tensor_copy(outT_sb[:, 1, :], ps_o[1][:, :]).then_inc(outT_ok, 1)

            def residual2(c):
                for pair in range(2):
                    n = 2 * c + pair
                    tiles = slice(2 * n, 2 * n + 2)
                    dve.wait_ge(out_ps, n + 1)
                    tt(x_sb[:, tiles, :], x_sb[:, tiles, :],
                       ps_out[pair][:, :].rearrange("p (j h) -> p j h", j=2), ALU.add).then_inc(res_ready, 1)

            multiply(NT, 0)
            take_out(0)
            multiply(NT + 1, 1)
            residual2(0)
            with dve.Fori(NPAIR + 1, 2 * NPAIR) as t:
                for u in range(2):
                    multiply(2 * t + u, u)
            take_out(1)
            residual2(1)


_IN = [("x", (TOKENS, D), "float32"), ("itok_BxS_13_99985", (TOKENS,), "int32"), ("ctx_2048", (EF, D), "float32"),
       ("L0_ffn_gate_W_packed", (N, D // 2), "int32"), ("L0_ffn_gate_scales", (N, D // BLOCK), "float32"),
       ("L0_ffn_up_W_packed", (N, D // 2), "int32"), ("L0_ffn_up_scales", (N, D // BLOCK), "float32"),
       ("L0_ffn_down_W_packed", (D, N // 2), "int32"), ("L0_ffn_down_scales", (D, N // BLOCK), "float32")]


def kernel(**inputs):
    import numpy as np
    import concourse.bacc as bacc
    from concourse.bass_utils import run_bass_kernel_spmd

    nc = bacc.Bacc("TRN2", target_bir_lowering=False, num_devices=1)
    arrays, args = {}, []
    for name, shape, dtype in _IN:
        a = np.ascontiguousarray(inputs[name]).reshape(shape)
        arrays[f"in_{name}"] = a
        args.append(nc.dram_tensor(f"in_{name}", a.shape, mybir.dt.from_np(a.dtype), kind="ExternalInput").ap())
    args.append(nc.dram_tensor("out_x", (TOKENS, D), mybir.dt.float32, kind="ExternalOutput").ap())
    xattn_ffn(nc, *args)
    result = run_bass_kernel_spmd(nc, [arrays], core_ids=[0])
    return result.results[0]["out_x"].reshape(4, 256, 256)
```

```python
import concourse.bass as bass
from concourse import mybir
from contextlib import ExitStack

P = 128
TOKENS, D = 1024, 256
TT = TOKENS // P
KT = D // P
CHUNK = 512
CT = CHUNK // P
E = 4
EF = E * 256
QI = E * KT
EI = 2 * QI
PER_EXPERT = 12500 // E
EPS = 1e-5
WARM_UP = 10
N = 2048
NT = N // P
NPAIR = NT // 2
BLOCK = 32
FP4_SHIFT = 64.0

STORES = [slice(0, 2), slice(2, 4), slice(4, 6), slice(6, 7), slice(7, 8)]
EARLY = 2
LATE = NPAIR - EARLY
H_AT = {7: (2, 3), 15: (4,)}
W_AT = {8: 0, 9: 1, 12: 2, 14: 3}
MASK_AT = {4: 4, 5: 5, 6: 6, 7: 7}
C_AT = 2
STATS_AT = {2: (1, 0), 3: (1, 1), 10: (2, 0), 11: (2, 1)}
NORM_AT = {4: (1, 0), 5: (1, 1), 12: (2, 0), 13: (2, 1)}
INV_STD_AT = {3: 1, 11: 2}
RESIDUAL_AT = {9: 0, 10: 1}
DECODE_AT = {6: 0, 9: 1}


def xattn_ffn(nc, x, tok, ctx_w, gate_w, gate_s, up_w, up_s, down_w, down_s, out):
    fp32, f32r, bf16 = mybir.dt.float32, mybir.dt.float32r, mybir.dt.bfloat16
    i32, u16, fp8 = mybir.dt.int32, mybir.dt.uint16, mybir.dt.float8e4
    ALU, ACT = mybir.AluOpType, mybir.ActivationFunctionType
    ds = bass.ds

    stack = ExitStack()
    with stack:
        def sb(name, shape, dt):
            return stack.enter_context(nc.sbuf_tensor(name, shape, dt))

        def sem(name):
            return stack.enter_context(nc.semaphore(name))

        x_sb = sb("x_sb", [P, TT, D], fp32)
        ident = sb("ident", [P, P], fp32)
        neg_half = sb("neg_half", [P, TT], fp32)
        warm = sb("warm", [1, 2], fp32)
        stats = sb("stats", [P, TT, 6], fp32)
        mean_var = sb("mean_var", [P, TT, 2], fp32)
        var = sb("var", [P, TT], fp32)
        rstd = sb("rstd", [P, TT], fp32)
        ctx_sb = sb("ctx_sb", [P, TT * D], fp32)
        d_pk = sb("d_pk", [P, KT * N // 2], i32)
        words = CT * E * P // 2
        small = d_pk[0:TT, words:]
        below = small[:, 0:2 * P].bitcast(fp32).rearrange("j (k t) -> j k t", k=2)
        mask_row = small[:, 2 * P:4 * P].bitcast(bf16).rearrange("j (e t) -> j e t", e=E)
        pick = small[:, 4 * P:8 * P].bitcast(bf16).rearrange("k (j t) -> k j t", j=TT)
        mask = [half[:, 0:words].bitcast(bf16).rearrange("p (j e t) -> p j e t", j=CT, e=E)
                for half in (d_pk, ctx_sb)]
        outT_sb = ctx_sb[:, 0:KT * CHUNK].rearrange("p (h t) -> p h t", h=KT)
        h_sb = sb("h_sb", [P, CT, D], fp32)
        cT_hi = sb("cT_hi", [P, KT, EF], f32r)
        cT_lo = sb("cT_lo", [P, KT, EF], f32r)
        hT_hi = sb("hT_hi", [P, KT, TOKENS], f32r)
        hT_lo = sb("hT_lo", [P, KT, TOKENS], f32r)
        act_sb = sb("act_sb", [P, 2, CHUNK], fp32)
        zeros = act_sb[:, 0, 0:CHUNK // 2].bitcast(bf16)
        prod_sb = [sb("prod0", [P, CHUNK], fp32), sb("prod1", [P, CHUNK], fp32), None]
        prod_hi = sb("prod_hi", [P, 3, CHUNK], f32r)
        prod_lo = sb("prod_lo", [P, 3, CHUNK], f32r)
        gu_pk = sb("gu_pk", [P, 2, NT * 128], i32)
        gu_sc = sb("gu_sc", [P, 2, NPAIR, 16], fp32)
        d_sc = sb("d_sc", [P, KT * N // BLOCK], fp32)
        d_scx = sb("d_scx", [P, KT, 128], fp32)
        code_hi = sb("code_hi", [P, 512], u16)
        code_lh = sb("code_lh", [P, 512], u16)
        code_mag = sb("code_mag", [P, 512], u16)
        code_sgn = sb("code_sgn", [P, 512], u16)
        gu_code = sb("gu_code", [P, 512], u16)
        d_code = sb("d_code", [P, 256], u16)
        gu_nat = sb("gu_nat", [P, 2, 2, D], fp32)
        tok_sb = gu_nat[0:TT, 0, 0, 0:P].bitcast(i32)
        d_nat = sb("d_nat", [P, KT, 2, P], fp32)
        prod_sb[2] = d_nat[:, :, :, :].rearrange("p h i n -> p (h i n)")
        wgu_hi = sb("wgu_hi", [P, 2, KT, N], f32r)
        wgu_lo = sb("wgu_lo", [P, 2, KT, N], f32r)
        wd_hi = sb("wd_hi", [P, NT * D], f32r)
        wd_lo = sb("wd_lo", [P, NT * D], f32r)

        bank = [stack.enter_context(nc.psum_tensor(f"bank{b}", [P, 512], fp32)) for b in range(8)]
        ps_z = bank[0:2]
        ps_y = (bank[4:6], bank[2:4])
        ps_gate, ps_up, ps_o = (bank[0], bank[2]), (bank[1], bank[3]), bank[4:6]
        ps_h, ps_w = bank[6], bank[7]
        ps_mask = bank[4:6] + bank[2:4] + bank[2:4] * 2
        ps_out = (bank[6], bank[7])

        s_tok = sem("s_tok")
        s_x, s_ctx = [sem("s_x0"), sem("s_x1"), sem("s_x2")], [sem("s_ctx0"), sem("s_ctx1")]
        s_gusc, s_dsc = sem("s_gusc"), sem("s_dsc")
        s_gupk, s_dpk = [sem("s_gupk0"), sem("s_gupk1")], sem("s_dpk")
        s_out = [sem(f"s_out{n}") for n in range(len(STORES))]
        warm_ok = sem("warm_ok")
        pick_ok, ident_ok, pow_ok = sem("pick_ok"), sem("ident_ok"), sem("pow_ok")
        scales_ok = sem("scales_ok")
        mask_step, mask_rows = sem("mask_step"), sem("mask_rows")
        mask_ps, mask_ok = sem("mask_ps"), sem("mask_ok")
        ln_step = sem("ln_step")
        var_ready = sem("var_ready")
        rstd_ready = sem("rstd_ready")
        cT_ps, cT_hi_ok, cT_lo_ok = sem("cT_ps"), sem("cT_hi_ok"), sem("cT_lo_ok")
        h_ready = sem("h_ready")
        h_ps, h_hi_ok, h_lo_ok = sem("h_ps"), sem("h_hi_ok"), sem("h_lo_ok")
        z_ready = sem("z_ready")
        silu_ready = sem("silu_ready")
        a_ready = sem("a_ready")
        am_ready = sem("am_ready")
        a_hi_ok, a_lo_ok = sem("a_hi_ok"), sem("a_lo_ok")
        y_done = sem("y_done")
        x1_ready = sem("x1_ready")
        gu_step, d_step = sem("gu_step"), sem("d_step")
        gu_codes, d_codes = sem("gu_codes"), sem("d_codes")
        gu_nat_ok, d_nat_ok = sem("gu_nat_ok"), sem("d_nat_ok")
        w_ps, w_hi_ok, w_lo_ok = sem("w_ps"), sem("w_hi_ok"), sem("w_lo_ok")
        gate_ready, up_ready = sem("gate_ready"), sem("up_ready")
        gelu_ready = sem("gelu_ready")
        inter_ready = sem("inter_ready")
        i_hi_ok, i_lo_ok = sem("i_hi_ok"), sem("i_lo_ok")
        last_lo_ok = sem("last_lo_ok")
        o_ready = sem("o_ready")
        outT0_ok, outT1_ok = sem("outT0_ok"), sem("outT1_ok")
        out_ps = sem("out_ps")
        res_ready = sem("res_ready")

        def piece_gu_late(t, m):
            return 2 * EARLY + 3 * t + 1 + m

        def piece_d_early(t):
            return 2 * EARLY + 3 * t

        def piece_d_late(t):
            return 2 * EARLY + 2 * LATE + t

        def piece_d(t):
            return piece_d_early(t) if t < LATE else piece_d_late(t)

        def h_bank(piece):
            return ps_w if piece in (1, 3) else ps_h

        def gu_bank(m, piece):
            return ps_h if m == 1 and piece >= 2 * EARLY else ps_w

        def finished(batch, half):
            t0 = CT * (batch % 2)
            return slice(2 * half, 2 * half + 2) if batch == 0 else slice(t0, t0 + CT)

        x_v = x.rearrange("(j p) d -> p j d", p=P)
        out_v = out.rearrange("(j p) d -> p j d", p=P)
        chunk_cols = [slice(c * CHUNK, (c + 1) * CHUNK) for c in range(2)]
        block = stack.enter_context(nc.Block())

        @block.sync
        def _(sp):
            ctx_v = ctx_w.rearrange("(b p) c -> p b c", p=P)
            ctx_blocks = ctx_sb[:, :].rearrange("p (b c) -> p b c", b=TT)
            for half in range(2):
                tiles = slice(2 * half, 2 * half + 2)
                sp.dma_start(x_sb[:, tiles, :], x_v[:, tiles, :]).then_inc(s_x[half], 16)
            sp.dma_start(tok_sb[:, :], tok.rearrange("(j p) -> j p", p=P)).then_inc(s_tok, 16)
            for half in range(2):
                blocks = slice(CT * half, CT * half + CT)
                sp.dma_start(ctx_blocks[:, blocks, :], ctx_v[:, blocks, :]).then_inc(s_ctx[half], 16)
            sp.dma_start(x_sb[:, CT:TT, :], x_v[:, CT:TT, :]).then_inc(s_x[2], 16)
            for m, s in enumerate((gate_s, up_s)):
                sp.dma_start(gu_sc[:, m, :, :],
                             s.rearrange("(p g i) b -> p g (i b)", g=NPAIR, i=2)).then_inc(s_gusc, 16)
            sp.dma_start(d_sc[:, :].rearrange("p (h b) -> p h b", h=KT),
                         down_s.rearrange("(h p) b -> p h b", p=P)).then_inc(s_dsc, 16)
            for part in range(2):
                cols = slice(part * N // 2, (part + 1) * N // 2)
                for m, w in enumerate((gate_w, up_w)):
                    sp.dma_start(gu_pk[:, m, cols],
                                 w.rearrange("(p i) c -> p (i c)", i=NT)[:, cols]).then_inc(s_gupk[part], 16)
            sp.wait_ge(mask_ok, TT)
            sp.wait_ge(am_ready, QI)
            sp.dma_start(d_pk[:, :].rearrange("p (h c) -> p h c", h=KT),
                         down_w.rearrange("(h p) c -> p h c", p=P)).then_inc(s_dpk, 16)
            for n, tiles in enumerate(STORES):
                sp.wait_ge(res_ready, n + 1)
                sp.dma_start(out_v[:, tiles, :], x_sb[:, tiles, :]).then_inc(s_out[n], 16)
            for n in range(len(STORES)):
                sp.wait_ge(s_out[n], 16)

        @block.gpsimd
        def _(pool):
            nc.gpsimd.memset(zeros[:, :], 0.0).then_inc(warm_ok, 1)
            nc.gpsimd.memset(pick[:, :, :], 0.0).then_inc(pick_ok, 1)
            nc.gpsimd.memset(ident[:, :], 0.0).then_inc(ident_ok, 1)
            nc.gpsimd.memset(neg_half[:, :], -0.5).then_inc(pow_ok, 1)
            pool.wait_ge(pick_ok, 1)
            nc.gpsimd.affine_select(out=pick[:, :, :], in_=pick[:, :, :], compare_op=ALU.not_equal, fill=1.0,
                                    base=0, pattern=[[-1, TT], [0, P]], channel_multiplier=1).then_inc(pick_ok, 1)
            pool.wait_ge(ident_ok, 1)
            nc.gpsimd.affine_select(out=ident[:, :], in_=ident[:, :], compare_op=ALU.not_equal, fill=1.0,
                                    base=0, pattern=[[-1, P]], channel_multiplier=1).then_inc(ident_ok, 1)
            pool.wait_ge(pow_ok, 1)

            def inv_std(batch, half=1):
                pool.wait_ge(var_ready, half + 1 if batch == 0 else batch + 2)
                t = finished(batch, half)
                nc.gpsimd.tensor_tensor(rstd[:, t], var[:, t], neg_half[:, t], ALU.pow).then_inc(rstd_ready, 1)

            def masked(n):
                c, e = n // QI, n % QI // KT
                pool.wait_ge(a_ready, n + 1)
                if n % QI == 0:
                    pool.wait_ge(mask_ok, CT * (c + 1))
                item = prod_sb[n % 3][:, :].rearrange("p (j t) -> p j t", j=CT)
                nc.gpsimd.tensor_tensor(item, item, mask[c][:, :, e, :],
                                        ALU.mult).then_inc(am_ready, 1)

            def dequant_gu(g):
                pool.wait_ge(gu_codes, g + 1)
                for m in range(2):
                    nc.gpsimd.tensor_tensor(
                        gu_nat[:, m, :, :].rearrange("p i (b c) -> p (i b) c", c=BLOCK),
                        gu_code[:, 256 * m:256 * (m + 1)].bitcast(fp8).rearrange("p (b c) -> p b c", c=BLOCK),
                        gu_sc[:, m, g, :].unsqueeze(2).to_broadcast([P, 16, BLOCK]),
                        ALU.mult).then_inc(gu_nat_ok, 1)

            def dequant_d(g):
                pool.wait_ge(d_codes, g + 1)
                nc.gpsimd.tensor_tensor(
                    d_nat[:, :, :, :].rearrange("p h i q -> p h q i"),
                    d_code[:, :].bitcast(fp8).rearrange("p (h q i) -> p h q i", h=KT, i=2),
                    d_scx[:, :, :].unsqueeze(3).to_broadcast([P, KT, P, 2]),
                    ALU.mult).then_inc(d_nat_ok, 1)

            def lo_inter(n, u):
                pool.wait_ge(i_hi_ok, n + 1)
                nc.gpsimd.tensor_tensor(prod_lo[:, 1 - u, :], prod_sb[1 - u][:, :], prod_hi[:, 1 - u, :].bitcast(fp32),
                                        ALU.subtract).then_inc(i_lo_ok, 1)

            inv_std(0, 0)
            inv_std(0, 1)
            masked(0)
            masked(1)
            masked(2)
            pool.wait_ge(s_gusc, 32)
            nc.gpsimd.tensor_scalar(gu_sc[:, :, :, :].rearrange("p m g b -> p (m g b)"),
                                    gu_sc[:, :, :, :].rearrange("p m g b -> p (m g b)"),
                                    FP4_SHIFT, 1.0, ALU.mult, ALU.mult).then_inc(scales_ok, 1)
            pool.wait_ge(s_dsc, 16)
            nc.gpsimd.tensor_scalar(d_scx[:, :, :].rearrange("p h (b s) -> p (h b) s", s=2),
                                    d_sc[:, :].unsqueeze(2).to_broadcast([P, KT * N // BLOCK, 2]),
                                    FP4_SHIFT, 1.0, ALU.mult, ALU.mult).then_inc(scales_ok, 1)
            pool.wait_ge(scales_ok, 2)
            for n in range(3, EI):
                masked(n)
                if n in DECODE_AT:
                    dequant_gu(DECODE_AT[n])
                if n in INV_STD_AT:
                    inv_std(INV_STD_AT[n])
            dequant_d(0)
            for t in range(NPAIR):
                if t < LATE:
                    dequant_gu(t + EARLY)
                lo_inter(2 * t, 0)
                if t + 1 < NPAIR:
                    dequant_d(t + 1)
                lo_inter(2 * t + 1, 1)
                if t == 1:
                    inv_std(3)
            with pool.Fori(NPAIR, 2 * NPAIR - 1) as t:
                for u in range(2):
                    lo_inter(2 * t + u, u)
            lo_inter(2 * NT - 2, 0)

        def products(psum, terms, first=True, last=True):
            n = 0
            for w_hi, w_lo, m_hi, m_lo in terms:
                for w, m in ((w_hi, m_hi), (w_hi, m_lo), (w_lo, m_hi)):
                    mm = nc.tensor.matmul(psum, w, m, start=first and n == 0,
                                          stop=last and n == 3 * len(terms) - 1, skip_group_check=True)
                    n += 1
            return mm

        @block.tensor
        def _(pe):
            def spread_mask(j):
                if j >= CT:
                    pe.wait_ge(mask_ok, j - 1)
                nc.tensor.matmul(ps_mask[j][:, :], pick[:, j, :], mask_row[:, :, :],
                                 start=True, stop=True).then_inc(mask_ps, 1)

            def transpose_c(half):
                pe.wait_ge(s_ctx[half], 16)
                for kt in range(KT):
                    for b in range(4):
                        r = (4 * half + b) * D + kt * P
                        mm = nc.tensor.transpose(bank[2 * half + kt][:, b * P:(b + 1) * P],
                                                 ctx_sb[:, r:r + P], ident[:, :])
                    mm.then_inc(cT_ps, 1)

            def transpose_h(piece, psum):
                pe.wait_ge(h_ready, CT * (piece // 2 + 1))
                if piece < 6:
                    pe.wait_ge(h_lo_ok, piece if piece > 3 else 2)
                for j in range(CT):
                    mm = nc.tensor.transpose(psum[:, j * P:(j + 1) * P],
                                             h_sb[:, j, piece % 2 * P:(piece % 2 + 1) * P], ident[:, :])
                mm.then_inc(h_ps, 1)

            def transpose_gu(g, m, piece):
                psum = gu_bank(m, piece)
                if piece:
                    pe.wait_ge(w_lo_ok, piece - 1 if psum is ps_h else piece)
                pe.wait_ge(gu_nat_ok, 2 * g + m + 1)
                for kt in range(KT):
                    for i in range(2):
                        c = (2 * kt + i) * P
                        mm = nc.tensor.transpose(psum[:, c:c + P], gu_nat[:, m, i, kt * P:(kt + 1) * P],
                                                 ident[:, :])
                mm.then_inc(w_ps, 1)

            def transpose_d(g, piece):
                pe.wait_ge(w_lo_ok, piece - 1 if g and g <= LATE else piece)
                pe.wait_ge(d_nat_ok, g + 1)
                for i in range(2):
                    for hb in range(KT):
                        c = (2 * i + hb) * P
                        mm = nc.tensor.transpose(ps_w[:, c:c + P], d_nat[:, hb, i, :], ident[:, :])
                mm.then_inc(w_ps, 1)

            def expert_in(n):
                c, q = n // QI, n % QI
                if n >= 2:
                    pe.wait_ge(a_ready, n - 1)
                for kt in range(KT):
                    if n == QI:
                        pe.wait_ge(h_lo_ok, KT + kt + 1)
                    mm = products(ps_z[n % 2][:, :],
                                  [(cT_hi[:, kt, q * P:(q + 1) * P], cT_lo[:, kt, q * P:(q + 1) * P],
                                    hT_hi[:, kt, chunk_cols[c]], hT_lo[:, kt, chunk_cols[c]])],
                                  first=kt == 0, last=kt == KT - 1)
                mm.then_inc(z_ready, 1)

            def first_expert_in():
                def part(w, m, kt, start=False, stop=False):
                    return nc.tensor.matmul(ps_z[0][:, :], w[:, kt, 0:P], m[:, kt, chunk_cols[0]],
                                            start=start, stop=stop)
                for kt in range(KT):
                    pe.wait_ge(cT_lo_ok, kt + 1)
                    pe.wait_ge(h_hi_ok, kt + 1)
                    part(cT_hi, hT_hi, kt, start=kt == 0)
                    part(cT_lo, hT_hi, kt)
                for kt in range(KT):
                    pe.wait_ge(h_lo_ok, kt + 1)
                    mm = part(cT_hi, hT_lo, kt, stop=kt == KT - 1)
                mm.then_inc(z_ready, 1)

            def expert_out(n):
                c, e, f = n // QI, n % QI // KT, n % KT
                pe.wait_ge(a_lo_ok, n + 1)
                for j in range(CT):
                    cols = slice(j * P, (j + 1) * P)
                    mm = products(ps_y[c][j // 2][:, j % 2 * D:(j % 2 + 1) * D],
                                  [(prod_hi[:, n % 3, cols], prod_lo[:, n % 3, cols],
                                    cT_hi[:, f, e * D:(e + 1) * D], cT_lo[:, f, e * D:(e + 1) * D])],
                                  first=n % QI == 0 and j % 2 == 0, last=n % QI == QI - 1)
                mm.then_inc(y_done, 1)

            def gate_up(n):
                c, i = n // NT, n % NT
                for m, (psum, ready) in enumerate(((ps_gate, gate_ready), (ps_up, up_ready))):
                    products(psum[n % 2][:, :],
                             [(wgu_hi[:, m, kt, i * P:(i + 1) * P], wgu_lo[:, m, kt, i * P:(i + 1) * P],
                               hT_hi[:, kt, chunk_cols[c]], hT_lo[:, kt, chunk_cols[c]]) for kt in range(KT)]
                             ).then_inc(ready, 1)

            def down(n):
                i, u = n % NT, 1 - n % 2
                w = [slice(i * D + hb * P, i * D + (hb + 1) * P) for hb in range(KT)]
                pe.wait_ge(i_hi_ok, n + 1)
                for hb in range(KT):
                    nc.tensor.matmul(ps_o[hb][:, :], wd_hi[:, w[hb]], prod_hi[:, u, :], start=i == 0, stop=False)
                    nc.tensor.matmul(ps_o[hb][:, :], wd_lo[:, w[hb]], prod_hi[:, u, :], start=False, stop=False)
                pe.wait_ge(i_lo_ok, n + 1)
                for hb in range(KT):
                    mm = nc.tensor.matmul(ps_o[hb][:, :], wd_hi[:, w[hb]], prod_lo[:, u, :], start=False,
                                          stop=i == NT - 1)
                    if i == NT - 1:
                        mm.then_inc(o_ready, 1)

            def last_down():
                halves = [slice(h * CHUNK // 2, (h + 1) * CHUNK // 2) for h in range(2)]
                w = [slice((NT - 1) * D + hb * P, (NT - 1) * D + (hb + 1) * P) for hb in range(KT)]
                for h, cols in enumerate(halves):
                    pe.wait_ge(i_hi_ok, 2 * NT + h)
                    for hb in range(KT):
                        for wd in (wd_hi, wd_lo):
                            nc.tensor.matmul(ps_o[hb][:, cols], wd[:, w[hb]], prod_hi[:, 0, cols],
                                             start=False, stop=False)
                pe.wait_ge(last_lo_ok, 2)
                for hb in range(KT):
                    nc.tensor.matmul(ps_o[hb][:, :], wd_hi[:, w[hb]], prod_lo[:, 0, :], start=False,
                                     stop=True).then_inc(o_ready, 1)

            def transpose_out(c):
                for pair in range(2):
                    pe.wait_ge(outT0_ok, 1 if c == 0 else pair + 2)
                    pe.wait_ge(outT1_ok, 1 if c == 0 else pair + 2)
                    for j in range(2):
                        for hb in range(KT):
                            t = (2 * pair + j) * P
                            mm = nc.tensor.transpose(ps_out[pair][:, (2 * j + hb) * P:(2 * j + hb + 1) * P],
                                                     outT_sb[:, hb, t:t + P], ident[:, :])
                    mm.then_inc(out_ps, 1)

            pe.wait_ge(warm_ok, 1)
            for n in range(WARM_UP):
                nc.tensor.matmul(bank[6][:, :], zeros[:, 0:P], zeros[:, :], start=True, stop=True)
            pe.wait_ge(ident_ok, 2)
            transpose_c(0)
            for j in range(CT):
                pe.wait_ge(h_ready, j + 1)
                for kt, psum in enumerate((ps_h, ps_w)):
                    mm = nc.tensor.transpose(psum[:, j * P:(j + 1) * P],
                                             h_sb[:, j, kt * P:(kt + 1) * P], ident[:, :])
                    if j == CT - 1:
                        mm.then_inc(h_ps, 1)
            first_expert_in()
            pe.wait_ge(pick_ok, 2)
            pe.wait_ge(mask_rows, 1)
            for j in range(CT):
                spread_mask(j)
            expert_in(1)
            for n in range(2, EI):
                if n == QI // 2:
                    pe.wait_ge(cT_lo_ok, 4)
                expert_in(n)
                if n == C_AT:
                    pe.wait_ge(mask_ok, CT)
                    transpose_c(1)
                for piece in H_AT.get(n, ()):
                    transpose_h(piece, h_bank(piece))
                if n >= 3:
                    expert_out(n - 3)
                if n in MASK_AT:
                    spread_mask(MASK_AT[n])
                if n in W_AT:
                    transpose_gu(W_AT[n] // 2, W_AT[n] % 2, W_AT[n])
            expert_out(EI - 3)
            expert_out(EI - 2)
            transpose_h(5, ps_h)
            expert_out(EI - 1)
            pe.wait_ge(h_lo_ok, 6)
            pe.wait_ge(w_lo_ok, 2)
            pe.wait_ge(a_ready, EI)
            for t in range(NPAIR):
                if t > 0:
                    pe.wait_ge(w_lo_ok, 2 * (t + 1) if t < EARLY else piece_gu_late(t - EARLY, 1) + 1)
                gate_up(2 * t)
                transpose_d(t, piece_d(t))
                if t > 0:
                    down(2 * t - 1)
                if t == 0:
                    pe.wait_ge(x1_ready, 4)
                if t == NPAIR - 1:
                    transpose_h(6, ps_h)
                    pe.wait_ge(w_lo_ok, piece_d(t) + 1)
                    transpose_h(7, ps_w)
                gate_up(2 * t + 1)
                if t < LATE:
                    transpose_gu(t + EARLY, 0, piece_gu_late(t, 0))
                else:
                    pe.wait_ge(w_lo_ok, piece_d(t) + 1)
                down(2 * t)
                if t < LATE:
                    transpose_gu(t + EARLY, 1, piece_gu_late(t, 1))
            pe.wait_ge(h_lo_ok, 8)
            for n in range(NT, 2 * NT):
                gate_up(n)
                if n == NT + 1:
                    transpose_out(0)
                down(n - 1)
            last_down()
            transpose_out(1)

        @block.scalar
        def _(act):
            def hi_part(dst, src):
                return nc.scalar.activation(dst, src, ACT.Copy)

            def take_mask(j):
                act.wait_ge(mask_ps, j + 1)
                nc.scalar.copy(mask[j // CT][:, j % CT, :, :].rearrange("p e t -> p (e t)"),
                               ps_mask[j][:, :]).then_inc(mask_ok, 1)

            def hi_h(piece, psum):
                act.wait_ge(h_ps, piece + 1)
                hi_part(hT_hi[:, piece % 2, chunk_cols[piece // 2 % 2]], psum[:, :]).then_inc(h_hi_ok, 1)

            def hi_c(half, kt):
                act.wait_ge(cT_ps, 2 * half + kt + 1)
                hi_part(cT_hi[:, kt, half * 512:half * 512 + 512], bank[2 * half + kt][:, :]).then_inc(cT_hi_ok, 1)

            def silu(n):
                act.wait_ge(z_ready, n + 1)
                nc.scalar.activation(act_sb[:, n % 2, :], ps_z[n % 2][:, :], ACT.Silu).then_inc(silu_ready, 1)

            def hi_a(n):
                act.wait_ge(am_ready, n + 1)
                if n >= 3:
                    act.wait_ge(y_done, n - 2)
                hi_part(prod_hi[:, n % 3, :], prod_sb[n % 3][:, :]).then_inc(a_hi_ok, 1)

            def hi_gu(g, m, piece, psum=ps_w):
                act.wait_ge(w_ps, piece + 1)
                hi_part(wgu_hi[:, m, :, ds(g * D, D)],
                        psum[:, :].rearrange("p (k n) -> p k n", k=KT)).then_inc(w_hi_ok, 1)

            def hi_d(g, piece):
                act.wait_ge(w_ps, piece + 1)
                hi_part(wd_hi[:, ds(g * 2 * D, 2 * D)], ps_w[:, :]).then_inc(w_hi_ok, 1)

            def gelu(n, u):
                act.wait_ge(gate_ready, n + 1)
                nc.scalar.activation(act_sb[:, u, :], ps_gate[u][:, :],
                                     ACT.Gelu_apprx_tanh).then_inc(gelu_ready, 1)

            def hi_inter(n, u):
                act.wait_ge(inter_ready, n + 1)
                hi_part(prod_hi[:, 1 - u, :], prod_sb[1 - u][:, :]).then_inc(i_hi_ok, 1)

            def take_out():
                act.wait_ge(o_ready, 1)
                nc.scalar.copy(outT_sb[:, 0, :], ps_o[0][:, :]).then_inc(outT0_ok, 1)

            def last_item():
                halves = [slice(h * CHUNK // 2, (h + 1) * CHUNK // 2) for h in range(2)]
                gelu(2 * NT - 1, 1)
                for h, cols in enumerate(halves):
                    act.wait_ge(inter_ready, 2 * NT + h)
                    hi_part(prod_hi[:, 0, cols], prod_sb[0][:, cols]).then_inc(i_hi_ok, 1)
                act.wait_ge(o_ready, KT + 1)
                for cols in halves:
                    nc.scalar.copy(outT_sb[:, 0, cols], ps_o[0][:, cols]).then_inc(outT0_ok, 1)

            act.wait_ge(pow_ok, 1)
            nc.scalar.activation(warm[:, 0:1], neg_half[0:1, 0:1], ACT.Silu)
            hi_c(0, 0)
            hi_c(0, 1)
            hi_h(0, ps_h)
            hi_h(1, ps_w)
            silu(0)
            for j in range(CT):
                take_mask(j)
            silu(1)
            hi_a(0)
            for n in range(2, EI):
                silu(n)
                for piece in H_AT.get(n, ()):
                    hi_h(piece, h_bank(piece))
                if n == C_AT:
                    hi_c(1, 0)
                    hi_c(1, 1)
                hi_a(n - 1)
                if n in MASK_AT:
                    take_mask(MASK_AT[n])
                if n in W_AT:
                    hi_gu(W_AT[n] // 2, W_AT[n] % 2, W_AT[n])
            hi_a(EI - 1)
            hi_h(5, ps_h)
            nc.scalar.activation(warm[:, 1:2], neg_half[0:1, 0:1], ACT.Gelu_apprx_tanh)

            def chunk0_pair(t, early, last=False):
                gelu(2 * t, 0)
                hi_d(t, piece_d_early(t) if early else piece_d_late(t))
                hi_inter(2 * t, 0)
                if last:
                    hi_h(6, ps_h)
                    hi_h(7, ps_w)
                gelu(2 * t + 1, 1)
                if early:
                    hi_gu(t + EARLY, 0, piece_gu_late(t, 0))
                hi_inter(2 * t + 1, 1)
                if early:
                    hi_gu(t + EARLY, 1, piece_gu_late(t, 1), ps_h)

            with act.Fori(0, LATE) as t:
                chunk0_pair(t, True)
            with act.Fori(LATE, NPAIR - 1) as t:
                chunk0_pair(t, False)
            chunk0_pair(NPAIR - 1, False, last=True)

            gelu(NT, 0)
            hi_inter(NT, 0)
            take_out()
            gelu(NT + 1, 1)
            hi_inter(NT + 1, 1)
            with act.Fori(NPAIR + 1, 2 * NPAIR - 1) as t:
                for u in range(2):
                    gelu(2 * t + u, u)
                    hi_inter(2 * t + u, u)
            gelu(2 * NT - 2, 0)
            hi_inter(2 * NT - 2, 0)
            last_item()

        @block.vector
        def _(dve):
            tt, ts, stt = nc.vector.tensor_tensor, nc.vector.tensor_scalar, nc.vector.scalar_tensor_tensor

            def lo_part(dst, src, hi):
                return tt(dst, src, hi.bitcast(fp32), ALU.subtract)

            def ln_stats(batch, half):
                t0, base = CT * (batch % 2), 8 * batch
                for j in range(t0 + 2 * half, t0 + 2 * half + 2):
                    nc.vector.bn_stats(stats[:, j, :], x_sb[:, j, :]).then_inc(ln_step, 1)
                dve.wait_ge(ln_step, base + 4 * half + 2)
                for j in range(t0 + 2 * half, t0 + 2 * half + 2):
                    nc.vector.bn_aggr(mean_var[:, j, :], stats[:, j, :]).then_inc(ln_step, 1)
                if batch == 0 or half == 1:
                    dve.wait_ge(ln_step, base + 4 * half + 4)
                    tiles = finished(batch, half)
                    ts(var[:, tiles], mean_var[:, tiles, 1], EPS, None, ALU.add).then_inc(var_ready, 1)

            def normalise(batch, half):
                dve.wait_ge(rstd_ready, half + 1 if batch == 0 else batch + 2)
                for k in (2 * half, 2 * half + 1):
                    j = CT * (batch % 2) + k
                    ts(h_sb[:, k, :], x_sb[:, j, :], mean_var[:, j, 0:1], rstd[:, j:j + 1],
                       ALU.subtract, ALU.mult).then_inc(h_ready, 1)

            def lo_h(piece, psum):
                dve.wait_ge(h_hi_ok, piece + 1)
                kt, cols = piece % 2, chunk_cols[piece // 2 % 2]
                lo_part(hT_lo[:, kt, cols], psum[:, :], hT_hi[:, kt, cols]).then_inc(h_lo_ok, 1)

            def lo_c(half, kt):
                dve.wait_ge(cT_hi_ok, 2 * half + kt + 1)
                cols = slice(half * 512, half * 512 + 512)
                lo_part(cT_lo[:, kt, cols], bank[2 * half + kt][:, :], cT_hi[:, kt, cols]).then_inc(cT_lo_ok, 1)

            def gated(n):
                if n >= 3:
                    dve.wait_ge(a_lo_ok, n - 2)
                dve.wait_ge(silu_ready, n + 1)
                tt(prod_sb[n % 3][:, :], act_sb[:, n % 2, :], ps_z[n % 2][:, :], ALU.mult).then_inc(a_ready, 1)

            def lo_a(n):
                dve.wait_ge(a_hi_ok, n + 1)
                lo_part(prod_lo[:, n % 3, :], prod_sb[n % 3][:, :], prod_hi[:, n % 3, :]).then_inc(a_lo_ok, 1)

            def residual1(c, pair):
                dve.wait_ge(y_done, QI * (c + 1))
                tiles = slice(CT * c + 2 * pair, CT * c + 2 * pair + 2)
                tt(x_sb[:, tiles, :], x_sb[:, tiles, :],
                   ps_y[c][pair][:, :].rearrange("p (j d) -> p j d", j=2), ALU.add).then_inc(x1_ready, 1)

            def decode(pk, n, shape, out_code, step, done, g):
                def v(tensor):
                    return tensor[:, 0:n].rearrange(shape[0], **shape[1])
                nib_hi, nib = v(code_hi), v(code_lh)
                shl, land, lor = ALU.logical_shift_left, ALU.bitwise_and, ALU.bitwise_or
                ts(nib_hi, pk, 4, 0x0f00, shl, land).then_inc(step, 1)
                dve.wait_ge(step, 4 * g + 1)
                stt(nib, pk, 0x000f, nib_hi, land, lor).then_inc(step, 1)
                dve.wait_ge(step, 4 * g + 2)
                ts(code_mag[:, 0:n], code_lh[:, 0:n], 2, 0x1c1c, shl, land).then_inc(step, 1)
                ts(code_sgn[:, 0:n], code_lh[:, 0:n], 4, 0x8080, shl, land).then_inc(step, 1)
                dve.wait_ge(step, 4 * g + 4)
                tt(out_code, code_mag[:, 0:n], code_sgn[:, 0:n], lor).then_inc(done, 1)

            gu_half = gu_pk[:, :, :].bitcast(u16).rearrange("p m (g c two) -> p m g c two", g=NPAIR, two=2)
            d_half = d_pk[:, :].bitcast(u16).rearrange("p (h q g two) -> p h g q two", h=KT, g=NPAIR, two=2)

            def decode_gu(g):
                decode(gu_half[:, :, ds(g, 1), :, 0], 512, ("p (m o c) -> p m o c", dict(m=2, o=1)),
                       gu_code[:, :], gu_step, gu_codes, g)

            def decode_d(g):
                decode(d_half[:, :, ds(g, 1), :, 0], 256, ("p (h o q) -> p h o q", dict(h=KT, o=1)),
                       d_code[:, :], d_step, d_codes, g)

            def lo_gu(g, m, piece, psum=ps_w):
                dve.wait_ge(w_hi_ok, piece + 1)
                cols = ds(g * D, D)
                lo_part(wgu_lo[:, m, :, cols], psum[:, :].rearrange("p (k n) -> p k n", k=KT),
                        wgu_hi[:, m, :, cols]).then_inc(w_lo_ok, 1)

            def lo_d(g, piece):
                dve.wait_ge(w_hi_ok, piece + 1)
                cols = ds(g * 2 * D, 2 * D)
                lo_part(wd_lo[:, cols], ps_w[:, :], wd_hi[:, cols]).then_inc(w_lo_ok, 1)

            for half in range(2):
                dve.wait_ge(s_x[half], 16)
                ln_stats(0, half)
            dve.wait_ge(s_tok, 16)
            for k in range(2):
                ts(below[:, k, :], tok_sb[:, :], float((k + 2) * PER_EXPERT), None,
                   ALU.is_lt).then_inc(mask_step, 1)
            ts(mask_row[:, 0, :], tok_sb[:, :], float(PER_EXPERT), None, ALU.is_lt)
            ts(mask_row[:, 3, :], tok_sb[:, :], float(3 * PER_EXPERT), None, ALU.is_ge)
            normalise(0, 0)
            normalise(0, 1)
            for kt in range(KT):
                lo_c(0, kt)
            for kt, psum in enumerate((ps_h, ps_w)):
                lo_h(kt, psum)
            dve.wait_ge(mask_step, 2)
            for k in range(2):
                op = stt(mask_row[:, k + 1, :], tok_sb[:, :], float((k + 1) * PER_EXPERT), below[:, k, :],
                         ALU.is_ge, ALU.mult)
            op.then_inc(mask_rows, 1)
            gated(0)
            for n in range(1, EI):
                gated(n)
                for piece in H_AT.get(n, ()):
                    lo_h(piece, h_bank(piece))
                if n == C_AT:
                    lo_c(1, 0)
                    lo_c(1, 1)
                lo_a(n - 1)
                if n in W_AT:
                    lo_gu(W_AT[n] // 2, W_AT[n] % 2, W_AT[n])
                if n in DECODE_AT:
                    if DECODE_AT[n] == 0:
                        dve.wait_ge(s_gupk[0], 32)
                    decode_gu(DECODE_AT[n])
                if n in RESIDUAL_AT:
                    residual1(0, RESIDUAL_AT[n])
                if n in STATS_AT:
                    if STATS_AT[n] == (1, 0):
                        dve.wait_ge(s_x[2], 16)
                    if STATS_AT[n] == (2, 0):
                        dve.wait_ge(x1_ready, 2)
                    ln_stats(*STATS_AT[n])
                if n in NORM_AT:
                    normalise(*NORM_AT[n])
            dve.wait_ge(s_dpk, 16)
            decode_d(0)
            lo_a(EI - 1)
            lo_h(5, ps_h)
            dve.wait_ge(s_gupk[1], 32)

            def multiply(n, u):
                dve.wait_ge(gelu_ready, n + 1)
                dve.wait_ge(up_ready, n + 1)
                tt(prod_sb[1 - u][:, :], act_sb[:, u, :], ps_up[u][:, :], ALU.mult).then_inc(inter_ready, 1)

            def chunk0_pair(t, early, first=False, last=False):
                if first:
                    residual1(1, 0)
                    residual1(1, 1)
                if early:
                    decode_gu(t + EARLY)
                multiply(2 * t, 0)
                lo_d(t, piece_d_early(t) if early else piece_d_late(t))
                if not last:
                    decode_d(t + 1)
                else:
                    lo_h(6, ps_h)
                    lo_h(7, ps_w)
                multiply(2 * t + 1, 1)
                if early:
                    lo_gu(t + EARLY, 0, piece_gu_late(t, 0))
                    lo_gu(t + EARLY, 1, piece_gu_late(t, 1), ps_h)

            chunk0_pair(0, True, first=True)
            dve.wait_ge(x1_ready, 4)
            ln_stats(3, 0)
            chunk0_pair(1, True)
            ln_stats(3, 1)
            chunk0_pair(2, True)
            normalise(3, 0)
            normalise(3, 1)
            with dve.Fori(3, LATE) as t:
                chunk0_pair(t, True)
            with dve.Fori(LATE, NPAIR - 1) as t:
                chunk0_pair(t, False)
            chunk0_pair(NPAIR - 1, False, last=True)

            def take_out():
                dve.wait_ge(o_ready, 2)
                nc.vector.tensor_copy(outT_sb[:, 1, :], ps_o[1][:, :]).then_inc(outT1_ok, 1)

            def last_item():
                halves = [slice(h * CHUNK // 2, (h + 1) * CHUNK // 2) for h in range(2)]
                dve.wait_ge(gelu_ready, 2 * NT)
                dve.wait_ge(up_ready, 2 * NT)
                for cols in halves:
                    tt(prod_sb[0][:, cols], act_sb[:, 1, cols], ps_up[1][:, cols], ALU.mult).then_inc(inter_ready, 1)
                for h, cols in enumerate(halves):
                    dve.wait_ge(i_hi_ok, 2 * NT + h)
                    lo_part(prod_lo[:, 0, cols], prod_sb[0][:, cols], prod_hi[:, 0, cols]).then_inc(last_lo_ok, 1)
                dve.wait_ge(o_ready, KT + 2)
                for cols in halves:
                    nc.vector.tensor_copy(outT_sb[:, 1, cols], ps_o[1][:, cols]).then_inc(outT1_ok, 1)

            def residual2(c):
                for n, tiles in enumerate(STORES):
                    if tiles.start // CT == c:
                        pair, j = tiles.start // 2, tiles.start % 2
                        dve.wait_ge(out_ps, pair + 1)
                        mlp = ps_out[pair % 2][:, :].rearrange("p (j h) -> p j h", j=2)
                        tt(x_sb[:, tiles, :], x_sb[:, tiles, :], mlp[:, j:j + tiles.stop - tiles.start, :],
                           ALU.add).then_inc(res_ready, 1)

            multiply(NT, 0)
            take_out()
            multiply(NT + 1, 1)
            residual2(0)
            with dve.Fori(NPAIR + 1, 2 * NPAIR - 1) as t:
                for u in range(2):
                    multiply(2 * t + u, u)
            multiply(2 * NT - 2, 0)
            last_item()
            residual2(1)


_IN = [("x", (TOKENS, D), "float32"), ("itok_BxS_13_99985", (TOKENS,), "int32"), ("ctx_2048", (EF, D), "float32"),
       ("L0_ffn_gate_W_packed", (N, D // 2), "int32"), ("L0_ffn_gate_scales", (N, D // BLOCK), "float32"),
       ("L0_ffn_up_W_packed", (N, D // 2), "int32"), ("L0_ffn_up_scales", (N, D // BLOCK), "float32"),
       ("L0_ffn_down_W_packed", (D, N // 2), "int32"), ("L0_ffn_down_scales", (D, N // BLOCK), "float32")]


def kernel(**inputs):
    import numpy as np
    import concourse.bacc as bacc
    from concourse.bass_utils import run_bass_kernel_spmd

    nc = bacc.Bacc("TRN2", target_bir_lowering=False, num_devices=1)
    arrays, args = {}, []
    for name, shape, dtype in _IN:
        a = np.ascontiguousarray(inputs[name]).reshape(shape)
        arrays[f"in_{name}"] = a
        args.append(nc.dram_tensor(f"in_{name}", a.shape, mybir.dt.from_np(a.dtype), kind="ExternalInput").ap())
    args.append(nc.dram_tensor("out_x", (TOKENS, D), mybir.dt.float32, kind="ExternalOutput").ap())
    xattn_ffn(nc, *args)
    result = run_bass_kernel_spmd(nc, [arrays], core_ids=[0])
    return result.results[0]["out_x"].reshape(4, 256, 256)
```
